# Optimizing a Trainium2 kernel written in Bass

```python
import numpy as np
import jax
import jax.numpy as jnp

def _softmax(x, axis=-1):
    return jax.nn.softmax(x, axis=axis)

def _gelu(x):
    return jax.nn.gelu(x, approximate=True)

def _silu(x):
    return jax.nn.silu(x)

def _sigmoid(x):
    return jax.nn.sigmoid(x)

def _layernorm(x, axis=-1, eps=1e-05):
    m = jnp.mean(x, axis=axis, keepdims=True)
    v = jnp.var(x, axis=axis, keepdims=True)
    return (x - m) / jnp.sqrt(v + eps)

def _scatter_add(tgt, idx, src, axis=0):
    return tgt.at[idx].add(src)

def _segment_sum(src, seg, n):
    return jax.ops.segment_sum(src, seg, n)
kernel_name = 'mk_gnn_resnorm_d1_gnn_r8_42d599'

def setup_inputs(seed: int=0):
    np.random.seed(seed)
    _w = jnp.asarray

    def _rec_inputs():
        import jax
        import jax.numpy as jnp
        _gk = jax.random.key(seed)
        x = -0.000202 + 1 * jax.random.normal(jax.random.fold_in(_gk, 1), (6250, 128), jnp.float32)
        src = jax.random.randint(jax.random.fold_in(_gk, 2), (100000,), 0, 6250, jnp.int32)
        dst = jnp.minimum((6250 * jax.random.uniform(jax.random.fold_in(_gk, 3), (100000,)) ** 2.0).astype(jnp.int32), 49999)
        _o = jnp.argsort(dst, stable=True)
        src = src[_o]
        dst = dst[_o]
        return (x, src, dst)
    x, src, dst = _rec_inputs()

    def _L0_gnn_setup():
        import jax, jax.numpy as jnp
        import numpy as np
        N_NODES = 6250
        N_EDGES = 100000
        NODE_DIM = 128
        HIDDEN = 256

        def _glorot(key, shape):
            fan_in, fan_out = (shape[0], shape[1])
            lim = np.sqrt(6.0 / (fan_in + fan_out)).astype(np.float32)
            return jax.random.uniform(key, shape, jnp.float32, -lim, lim)
        key = jax.random.key(seed)
        ks = jax.random.split(key, 12)
        node_features = jax.random.normal(ks[0], (N_NODES, NODE_DIM), jnp.float32)
        edge_index = jax.random.randint(ks[1], (2, N_EDGES), 0, N_NODES, jnp.int64)
        return {'node_features': node_features, 'edge_index': edge_index, 'Wm1': _glorot(ks[2], (2 * NODE_DIM, HIDDEN)), 'bm1': jnp.zeros((HIDDEN,), jnp.float32), 'Wm2': _glorot(ks[3], (HIDDEN, HIDDEN)), 'bm2': jnp.zeros((HIDDEN,), jnp.float32), 'Wm3': _glorot(ks[4], (HIDDEN, NODE_DIM)), 'bm3': jnp.zeros((NODE_DIM,), jnp.float32), 'Wn1': _glorot(ks[5], (2 * NODE_DIM, HIDDEN)), 'bn1': jnp.zeros((HIDDEN,), jnp.float32), 'Wn2': _glorot(ks[6], (HIDDEN, NODE_DIM)), 'bn2': jnp.zeros((NODE_DIM,), jnp.float32)}
    _L0_gnn_all = _L0_gnn_setup()
    _L0_gnn_in = {k: v for k, v in _L0_gnn_all.items() if k in ('Wm1', 'bm1', 'Wm2', 'bm2', 'Wm3', 'bm3', 'Wn1', 'bn1', 'Wn2', 'bn2')}
    del _L0_gnn_all
    return {'x': x, 'src': src, 'dst': dst, 'L0_gnn_Wm1': _L0_gnn_in['Wm1'], 'L0_gnn_bm1': _L0_gnn_in['bm1'], 'L0_gnn_Wm2': _L0_gnn_in['Wm2'], 'L0_gnn_bm2': _L0_gnn_in['bm2'], 'L0_gnn_Wm3': _L0_gnn_in['Wm3'], 'L0_gnn_bm3': _L0_gnn_in['bm3'], 'L0_gnn_Wn1': _L0_gnn_in['Wn1'], 'L0_gnn_bn1': _L0_gnn_in['bn1'], 'L0_gnn_Wn2': _L0_gnn_in['Wn2'], 'L0_gnn_bn2': _L0_gnn_in['bn2']}

def reference(x, src, dst, L0_gnn_Wm1, L0_gnn_bm1, L0_gnn_Wm2, L0_gnn_bm2, L0_gnn_Wm3, L0_gnn_bm3, L0_gnn_Wn1, L0_gnn_bn1, L0_gnn_Wn2, L0_gnn_bn2):
    import jax
    import jax.numpy as jnp

    def _L0_gnn_ref(node_features, edge_index, Wm1, bm1, Wm2, bm2, Wm3, bm3, Wn1, bn1, Wn2, bn2):
        import jax, jax.numpy as jnp
        import numpy as np
        N_NODES = 6250
        N_EDGES = 100000
        NODE_DIM = 128
        HIDDEN = 256

        def _glorot(key, shape):
            fan_in, fan_out = (shape[0], shape[1])
            lim = np.sqrt(6.0 / (fan_in + fan_out)).astype(np.float32)
            return jax.random.uniform(key, shape, jnp.float32, -lim, lim)
        num_nodes = node_features.shape[0]
        row, col = (edge_index[0], edge_index[1])
        msg_in = jnp.concatenate([node_features[row], node_features[col]], axis=-1)
        h = jax.nn.relu(msg_in @ Wm1 + bm1)
        h = jax.nn.relu(h @ Wm2 + bm2)
        messages = h @ Wm3 + bm3
        agg = jax.ops.segment_sum(messages, col, num_segments=num_nodes)
        count = jax.ops.segment_sum(jnp.ones((messages.shape[0],), messages.dtype), col, num_segments=num_nodes)
        agg = agg / jnp.clip(count, 1.0)[:, None]
        node_in = jnp.concatenate([node_features, agg], axis=-1)
        upd = jax.nn.relu(node_in @ Wn1 + bn1) @ Wn2 + bn2
        return node_features + upd
    edge_index = jnp.stack([src, dst])
    x = _layernorm(x + _L0_gnn_ref(x, edge_index, L0_gnn_Wm1, L0_gnn_bm1, L0_gnn_Wm2, L0_gnn_bm2, L0_gnn_Wm3, L0_gnn_bm3, L0_gnn_Wn1, L0_gnn_bn1, L0_gnn_Wn2, L0_gnn_bn2), axis=-1)
    return x

_drawn_inputs = setup_inputs


def setup_inputs(seed=0):
    import zlib

    import numpy as np

    out = dict(_drawn_inputs(seed))
    spreads = {'L0_gnn_bm1': (0.0, 0.79),
     'L0_gnn_bm2': (0.0, 0.382),
     'L0_gnn_bm3': (0.0, 0.382),
     'L0_gnn_bn1': (0.0, 0.1),
     'L0_gnn_bn2': (0.0, 0.1)}
    factors = {}
    for name, (base, spread) in spreads.items():
        noise = np.random.default_rng([zlib.crc32(name.encode()), seed]).standard_normal(out[name].shape)
        drawn = base * np.exp(spread * noise) if base else spread * noise
        out[name] = jnp.asarray(drawn.astype(out[name].dtype))
    for name, factor in factors.items():
        out[name] = (out[name] * factor).astype(out[name].dtype)
    return out
```

```python
from contextlib import ExitStack

import numpy as np

import concourse.bass as bass
from concourse import mybir

F32 = mybir.dt.float32
F32R = mybir.dt.float32r
I32 = mybir.dt.int32
I16 = mybir.dt.int16
ALU = mybir.AluOpType
ACT = mybir.ActivationFunctionType
AX = mybir.AxisListType

P = 128
TB = 2
EB = TB * P
U = 4
EPS = 1e-5


def gnn_layer(nc, x, src, dst, Wm1, bm1, Wm2, bm2, Wm3, bm3, Wn1, bn1, Wn2, bn2, out):
    N, D = x.shape
    (E,) = src.shape
    H = Wm1.shape[1]
    KH = H // P
    NW = -(-N // P)
    NLAST = N - (NW - 1) * P
    NB = -(-E // EB)
    NB = -(-NB // U) * U
    GR = 4
    BG = NB // GR
    NI = NB // U
    PAD_DST = NW * P - 1
    GW = 4
    NG = -(-NW // GW)
    HC = H + 2
    assert D == P and H == 2 * P and BG <= P and NI >= 3 and NW >= 4 and NW * P > N

    a_table = nc.dram_tensor("a_table", [NW * P, H], F32, kind="Internal").ap()
    dst16_dram = nc.dram_tensor("dst16_dram", [NB, EB], I16, kind="Internal").ap()
    win_dram = nc.dram_tensor("win_dram", [NB, 2], I32, kind="Internal").ap()

    with ExitStack() as ctx:
        def sb(name, shape, dt):
            return ctx.enter_context(nc.sbuf_tensor(name, shape, dt))

        def sem(name):
            return ctx.enter_context(nc.semaphore(name))

        b_tab = sb("b_tab", [P, NW, 2, H], F32)
        agg = sb("agg", [P, NW * HC], F32)
        iota16 = sb("iota16", [P, NW * P], I16)
        node_id = sb("node_id", [P, NW], F32)
        src_idx = sb("src_idx", [P, NB * TB], I32)
        dst_col = sb("dst_col", [P, NB * TB], F32)
        win_row = sb("win_row", [1, 2 * (NB + 8)], I32)
        w2 = sb("w2", [P, 2, KH, H], F32R)
        b2_rows = sb("b2_rows", [2, 2 * H], F32R)
        ones2 = sb("ones2", [2, P], F32R)
        ident = sb("ident", [P, P], F32)
        a_edge = sb("a_edge", [P, U * TB, H], F32)
        idx_now = sb("idx_now", [P, U * TB], I32)
        zero_idx = sb("zero_idx", [P, TB], I32)
        dst_all = sb("dst_all", [P, 2, 2 * EB], I16)
        onehot_t = sb("onehot_t", [P, EB], F32R)
        b_win = sb("b_win", [P, 2, H], F32R)
        onehot = sb("onehot", [P, TB, P], F32R)
        h1 = sb("h1", [P, 2, 2, KH * EB], F32R)
        h2_hi = sb("h2_hi", [P, 2, TB, HC], F32R)
        h2_lo = sb("h2_lo", [P, 2, TB, H], F32R)

        bank = [ctx.enter_context(nc.psum_tensor(f"bank{i}", [P, 512], F32)) for i in range(8)]

        wab = h1[:, 0, :, :]
        xl = h1[:, 1, :, :]
        xh = h2_lo[:, :, :, :].rearrange("p s t h -> p s (t h)")
        b1_rows = b_win[0:2, :, :].rearrange("p a h -> p (a h)")
        edges_in = a_edge[:, :, :].rearrange("p a h -> p (a h)").bitcast(I32)

        class Carve:
            def __init__(self, region, limit):
                self.region, self.at, self.limit = region, 0, limit

            def __call__(self, *shape):
                cols = int(np.prod(shape))
                v = self.region[:, self.at:self.at + cols]
                self.at += cols
                assert self.at <= self.limit
                if len(shape) == 2:
                    return v.rearrange("p (a b) -> p a b", a=shape[0])
                if len(shape) == 3:
                    return v.rearrange("p (a b c) -> p a b c", a=shape[0], b=shape[1])
                return v

        carve = Carve(agg, NW * HC)
        w_stage = carve(4 * H)
        x_slot = carve(2, GW, D)
        a_out = carve(2, GW, H)
        edges_f = carve(2 * GR * EB)
        edges16 = carve(GR * EB // 2).bitcast(I16)
        rows_in = carve(2, H)
        rows_hi = carve(2, H)
        rows_lo = carve(2, H)
        minmax = carve(2 * GR)
        minmax_i = carve(2 * GR).bitcast(I32)
        win_i = carve(2 * GR).bitcast(I32)
        carve = Carve(b_tab[:, :, :, :].rearrange("p w a h -> p (w a h)"), NW * 2 * H)
        f_x = carve(NW, D)
        f_xs = carve(2, GW, D)
        f_cnt, f_rec = carve(2, GW), carve(2, GW)
        f_mean = carve(2, GW, HC)
        f_feat = carve(2, 3, GW * P)
        f_msg = carve(2, GW * P)
        f_hid = carve(2, KH, GW * P)
        f_y, f_out = carve(2, GW * D), carve(2, GW, D)
        f_bn, f_mv = carve(2, GW, 6), carve(2, GW, 2)
        f_ve, f_sd, f_rs = carve(2, GW), carve(2, GW), carve(2, GW)
        w3, wn1, wn2 = carve(KH, D), carve(2, H), carve(KH, D)
        bn1_col = carve(KH)
        f_bias_in, f_bias_hi, f_bias_lo = carve(2 * D), carve(2 * D), carve(2 * D)
        f_row = [h1[0:2, k, 0, :] for k in range(2)]
        bn2_rows = h1[0:2, 0, 1, :]
        b3_rows = h1[0:2, 1, 1, 0:D]

        s_w = sem("s_weights_loaded")
        s_edges = sem("s_edges_loaded")
        s_pad = sem("s_padding_set")
        s_zeros = sem("s_ident_zeroed")
        s_const = sem("s_constants")
        s_hi = sem("s_weights_hi")
        s_lo = sem("s_bias_parts")
        s_split = sem("s_weights_split")
        s_ef = sem("s_edges_as_float")
        s_mm = sem("s_min_max")
        s_wi = sem("s_min_max_int")
        s_win = sem("s_windows_found")
        s_d16 = sem("s_dst16_made")
        s_scr = sem("s_scratch_stored")
        s_row = sem("s_win_row_loaded")
        s_et = sem("s_edges_transposed")
        s_ec = sem("s_edge_columns")
        s_xs = [sem(f"s_x_in_slot{k}") for k in range(2)]
        s_xz = sem("s_last_x_zeroed")
        s_xt = sem("s_x_transposed")
        s_xh = sem("s_x_hi")
        s_xl = sem("s_x_lo")
        s_ab = sem("s_ab_product")
        s_ac = sem("s_a_copied")
        s_as = [sem(f"s_a_stored{k}") for k in range(2)]
        s_bh = sem("s_b_hi")
        s_bl = sem("s_b_lo")
        s_zero = sem("s_agg_zeroed")
        s_idx = sem("s_idx_copied")
        s_g = [sem(f"s_gathered{t}") for t in range(U * TB)]
        s_da = [sem(f"s_dst_all{c}") for c in range(2)]
        s_ta = sem("s_a_transposed")
        s_ot = sem("s_onehot_t_made")
        s_bw = sem("s_b_win_copied")
        s_ex = sem("s_expanded")
        s_h1h = sem("s_h1_hi")
        s_h1l = sem("s_h1_lo")
        s_w2 = sem("s_h2_product")
        s_h2h = sem("s_h2_hi")
        s_h2l = sem("s_h2_lo")
        s_oh = sem("s_onehot_made")
        s_sg = sem("s_segments_summed")
        s_end = sem("s_sums_complete")
        s_fz = sem("s_final_x_zeroed")
        s_fx = sem("s_final_loaded")
        s_f1 = sem("s_count_clamped")
        s_f2 = sem("s_count_inverted")
        s_fm = sem("s_mean")
        s_fxs = sem("s_final_x_in_slot")
        s_fbh = sem("s_final_bias_hi")
        s_fbl = sem("s_final_bias_lo")
        s_fbr = sem("s_final_bias_rows")
        s_fmt = sem("s_mean_transposed")
        s_fc = sem("s_features_copied")
        s_fcx = sem("s_final_x_copied")
        s_fr = sem("s_mask_row")
        s_fg = sem("s_message_product")
        s_fa = sem("s_message_copied")
        s_fh = sem("s_hidden_product")
        s_fhr = sem("s_hidden_relu")
        s_fu = sem("s_update_product")
        s_fy = sem("s_residual_added")
        s_fn = sem("s_bn_stats")
        s_fv = sem("s_mean_variance")
        s_fe = sem("s_variance_eps")
        s_fs = sem("s_std")
        s_fq = sem("s_std_inverted")
        s_fo = sem("s_normalised")
        s_fst = [sem(f"s_out_stored{k}") for k in range(2)]

        def groups(e, step, lag, ahead=0):
            first = lag + 2
            count = (NG - 1 - ahead - first) // 2
            for g in range(first):
                step(g, g % 2, g // 2)
            with e.Fori(0, count) as i:
                for k in range(2):
                    step(i * 2 + (first + k), (first + k) % 2, i + (first + k) // 2)
            for g in range(first + 2 * count, NG + lag):
                step(g, g % 2, g // 2)

        def size(g, back=0):
            if isinstance(g, int) and not 0 <= g - back < NG:
                return 0
            return NW - (NG - 1) * GW if isinstance(g, int) and g - back == NG - 1 else GW

        def used(g, back=0):
            return not isinstance(g, int) or g - back >= 2

        def load_x(e, g, n, to, done):
            whole = n if not (isinstance(g, int) and g == NG - 1) else n - 1
            if whole:
                e.dma_start(to[:, 0:whole, :], x[bass.ds(g * (GW * P), whole * P), :]
                            .rearrange("(w p) d -> p w d", p=P)).then_inc(done, 16)
            if whole < n:
                e.dma_start(to[0:NLAST, whole, :], x[N - NLAST:N, :]).then_inc(done, 16)

        def bodies(e, body):
            body(0)
            with e.Fori(1, NI - 1) as i:
                body(i)
            body(NI - 1)

        def there(i, k):
            return not isinstance(i, int) or 0 <= U * i + k < NB

        def load_windows(e, i):
            vals = nc.values_load_multi_w_load_instructions(
                win_row[0:1, bass.ds(i * (2 * U), 2 * (U + 4))], engines=[e.engine], min_val=0, max_val=NW - 1,
                skip_runtime_bounds_check_because="dst is a node's number")[1]
            return {k: (vals[2 * k + 4], vals[2 * k + 5]) for k in range(-2, U + 2)}

        def further(e, lo, hi, step):
            with e.If(lo < hi):
                with e.Fori(lo + 1, hi + 1) as w:
                    step(w)

        def steps(i):
            return range(U + 2) if isinstance(i, int) and i == NI - 1 else range(U)

        full = E // EB
        assert (GR - 1) * BG <= full
        loads = []
        for n in range(2):
            for g in range(GR):
                rows = min(full - g * BG, BG)
                if rows:
                    loads.append((n, g, 0, rows, EB))
            if E % EB:
                loads.append((n, GR - 1, rows, 1, E % EB))

        NPAIR = 2 * (NG - 1) + (size(NG - 1) + 1) // 2

        block = ctx.enter_context(nc.Block())

        @block.sync
        def _(sp):
            sp.wait_ge(s_pad, 2)
            for n, g, row, rows, edges in loads:
                at, e0 = (n * GR + g) * EB, (g * BG + row) * EB
                sp.dma_start(edges_in[row:row + rows, at:at + edges],
                             (dst, src)[n][e0:e0 + rows * edges].rearrange("(b e) -> b e", e=edges)
                             ).then_inc(s_edges, 16)
            for g in range(2):
                load_x(sp, g, GW, x_slot[:, g, :, :], s_xs[g])
            sp.wait_ge(s_win, 1)
            sp.wait_ge(s_d16, 1)
            for g in range(GR):
                sp.dma_start(win_dram[g * BG:(g + 1) * BG, :], win_i[0:BG, 2 * g:2 * g + 2]).then_inc(s_scr, 16)
                sp.dma_start(dst16_dram[g * BG:(g + 1) * BG, :],
                             edges16[0:BG, g * EB:(g + 1) * EB]).then_inc(s_scr, 16)
            sp.wait_ge(s_scr, 32 * GR)
            sp.dma_start(win_row[0:1, 4:4 + 2 * NB], win_dram.rearrange("(o b) c -> o (b c)", o=1)
                         ).then_inc(s_row, 16)

            def tables(g, k, half):
                if size(g) and used(g):
                    sp.wait_ge(s_xt, g - 1)
                    if size(g) < GW:
                        sp.wait_ge(s_xz, 1)
                    load_x(sp, g, size(g), x_slot[:, k, :, :], s_xs[k])
                n = size(g, 2)
                if n:
                    sp.wait_ge(s_ac, g * 2 - 2 if n > 2 else g * 2 - 3)
                    sp.dma_start(a_table[bass.ds((g - 2) * (GW * P), n * P), :]
                                 .rearrange("(w p) h -> p w h", p=P), a_out[:, k, 0:n, :]).then_inc(s_as[k], 16)
            groups(sp, tables, 2)

            def body(i):
                for c in range(2):
                    if there(i, -1):
                        sp.wait_ge(s_h1l, i * U + (2 * c - 2))
                    sp.dma_start(dst_all[:, c, :].rearrange("p (b e) -> p b e", b=2),
                                 dst16_dram[bass.ds(i * U + 2 * c, 2), :].partition_broadcast(P)
                                 ).then_inc(s_da[c], 16)
            bodies(sp, body)

            sp.wait_ge(s_end, 1)
            sp.dma_start(f_x[:, 0:NW - 1, :], x[0:(NW - 1) * P, :].rearrange("(w p) d -> p w d", p=P)
                         ).then_inc(s_fx, 16)
            sp.dma_start(w3, Wm3.rearrange("(k p) d -> p k d", p=P)).then_inc(s_fx, 16)
            sp.dma_start(wn1, Wn1.rearrange("(k p) d -> p k d", p=P)).then_inc(s_fx, 16)
            sp.dma_start(wn2, Wn2.rearrange("(k p) d -> p k d", p=P)).then_inc(s_fx, 16)
            sp.dma_start(f_bias_in[0:2, 0:D], bm3.partition_broadcast(2)).then_inc(s_fx, 16)
            sp.dma_start(f_bias_in[0:2, D:2 * D], bn2.partition_broadcast(2)).then_inc(s_fx, 16)
            for k in range(KH):
                sp.dma_start(bn1_col[:, k:k + 1], bn1[k * P:(k + 1) * P].rearrange("(p o) -> p o", o=1)
                             ).then_inc(s_fx, 16)
            sp.wait_ge(s_fz, 1)
            sp.dma_start(f_x[0:NLAST, NW - 1, :], x[(NW - 1) * P:N, :]).then_inc(s_fx, 16)

            def store_out(g, k, half):
                n = size(g)
                sp.wait_ge(s_fo, g + 1)
                whole = n - 1 if isinstance(g, int) and g == NG - 1 else n
                if whole:
                    sp.dma_start(out[bass.ds(g * (GW * P), whole * P), :].rearrange("(w p) d -> p w d", p=P),
                                 f_out[:, k, 0:whole, :]).then_inc(s_fst[k], 16)
                if whole < n:
                    sp.dma_start(out[N - NLAST:N, :], f_out[0:NLAST, k, whole, :]).then_inc(s_fst[k], 16)
            groups(sp, store_out, 0)
            last = (NG - 1) % 2
            for k in range(2):
                sp.wait_ge(s_fst[k], 16 * ((NG + 1 - k) // 2 + (k == last and size(NG - 1) > 1)))

        @block.gpsimd
        def _(pool):
            pool.memset(edges_in[:, (GR - 1) * EB:GR * EB], PAD_DST).then_inc(s_pad, 1)
            pool.memset(edges_in[:, (2 * GR - 1) * EB:2 * GR * EB], 0).then_inc(s_pad, 1)
            pool.memset(ident[:, :], 0.0).then_inc(s_zeros, 1)
            pool.wait_ge(s_zeros, 1)
            pool.affine_select(out=ident[:, :], in_=ident[:, :], compare_op=ALU.not_equal, fill=1.0,
                               base=0, pattern=[[-1, P]], channel_multiplier=1).then_inc(s_const, 1)
            pool.memset(ones2[:, :].bitcast(F32), 1.0).then_inc(s_const, 1)
            pool.memset(zero_idx[:, :], 0).then_inc(s_const, 1)
            pool.memset(h2_hi[:, :, :, H:HC].bitcast(F32), 1.0).then_inc(s_const, 1)
            pool.iota(node_id[:, :], pattern=[[P, NW]], base=0, channel_multiplier=1,
                      allow_small_or_imprecise_dtypes=True).then_inc(s_const, 1)
            pool.iota(iota16[:, :], pattern=[[1, NW * P]], base=0, channel_multiplier=0,
                      allow_small_or_imprecise_dtypes=True).then_inc(s_const, 1)
            pool.memset(win_row[0:1, 0:4], 0).then_inc(s_const, 1)
            pool.memset(win_row[0:1, 4 + 2 * NB:2 * (NB + 8)], 0).then_inc(s_const, 1)

            pool.wait_ge(s_xt, NG - 2)
            pool.memset(x_slot[:, (NG - 1) % 2, size(NG - 1) - 1, :], 0.0).then_inc(s_xz, 1)
            for k in range(2):
                pool.wait_ge(s_as[k], 16 * ((NG + 1 - k) // 2))
            pool.wait_ge(s_ec, 2 * GR)

            copied = pool.alloc_register("blocks_with_indices")
            pool.reg_mov(copied, 1)

            def copy_idx(i, k):
                at = k % U * TB
                v = src_idx[:, bass.ds(i * (U * TB) + k * TB, TB)]
                pool.tensor_tensor(idx_now[:, at:at + TB], v, zero_idx[:, :], ALU.add).then_inc(s_idx, 1)

            copy_idx(0, 0)

            def body(i):
                for k in range(U):
                    if there(i, k - U):
                        pool.wait_ge(s_ta, i * U + (k - U + 1))
                    if there(i, k + 1 - U):
                        for t in range(TB):
                            pool.wait_ge(s_g[(k + 1) % U * TB + t], i * 16 + 16 * ((k + 1) // U))
                    if there(i, k + 1):
                        pool.wait_ge(s_idx, copied)
                        copy_idx(i, k + 1)
                    else:
                        pool.wait_ge(s_idx, NB)
                    pool.reg_add(copied, copied, 1)
                    for t in range(k * TB, (k + 1) * TB):
                        pool.indirect_dma_start(a_edge[:, t, :], None, a_table,
                                                bass.IndirectOffsetOnAxis(ap=idx_now[:, t:t + 1], axis=0)
                                                ).then_inc(s_g[t], 16)
            bodies(pool, body)
            pool.wait_ge(s_end, 1)
            pool.memset(f_x[:, NW - 1, :], 0.0).then_inc(s_fz, 1)
            pool.wait_ge(s_fx, 16 * 9)

            def final(g, k, half):
                if used(g):
                    pool.wait_ge(s_fmt, g - 1)
                n = size(g)
                pool.tensor_copy(f_xs[:, k, 0:n, :], f_x[:, bass.ds(g * GW, n), :]).then_inc(s_fxs, 1)
            groups(pool, final, 0)

        @block.scalar
        def _(act):
            act.dma_start(w_stage[:, 0:2 * H].rearrange("p (k h) -> p k h", k=2),
                          Wm1.rearrange("(k p) h -> p k h", p=P)).then_inc(s_w, 16)
            act.dma_start(w_stage[:, 2 * H:4 * H].rearrange("p (k h) -> p k h", k=2),
                          Wm2.rearrange("(k p) h -> p k h", p=P)).then_inc(s_w, 16)
            act.dma_start(rows_in[0:2, 0, :], bm1.partition_broadcast(2)).then_inc(s_w, 16)
            act.dma_start(rows_in[0:2, 1, :], bm2.partition_broadcast(2)).then_inc(s_w, 16)
            act.wait_ge(s_w, 64)
            act.copy(wab[:, 0, :], w_stage[:, 0:2 * H]).then_inc(s_hi, 1)
            act.copy(w2[:, 0, :, :].rearrange("p k h -> p (k h)"), w_stage[:, 2 * H:4 * H]).then_inc(s_hi, 1)
            act.copy(rows_hi[0:2, :, :].bitcast(F32R), rows_in[0:2, :, :]).then_inc(s_hi, 1)

            def tables(g, k, half):
                n = size(g)
                if n:
                    act.wait_ge(s_xt, g + 1)
                    if used(g):
                        act.wait_ge(s_ab, g * 2 - 2)
                    act.copy(xh[:, k, 0:n * P], bank[k][:, 0:n * P]).then_inc(s_xh, 1)
                n = size(g, 1)
                for q in range((n + 1) // 2):
                    m = min(n - 2 * q, 2)
                    act.wait_ge(s_ab, g * 2 - 2 + (q + 1))
                    if used(g, 1) and q == 0:
                        act.wait_ge(s_as[1 - k], ((g - 1) // 2 if isinstance(g, int) else half - 1 + k) * 16)
                    act.copy(a_out[:, 1 - k, 2 * q:2 * q + m, :],
                             bank[2 + q][:, 0:m * H].rearrange("p (w h) -> p w h", h=H)).then_inc(s_ac, 1)
                    act.copy(b_tab[:, bass.ds(g * GW - GW + 2 * q, m), 0, :].bitcast(F32R),
                             bank[4 + q][:, 0:m * H].rearrange("p (w h) -> p w h", h=H)).then_inc(s_bh, 1)
            groups(act, tables, 1)
            act.wait_ge(s_bl, NPAIR)
            act.wait_ge(s_row, 16)
            pairs = act.alloc_register("expanded_pairs_act")
            act.reg_mov(pairs, 0)

            def copy_b(w):
                act.copy(b_win[:, :, :].rearrange("p a h -> p (a h)"),
                         b_tab[:, bass.ds(w, 1), :, :].rearrange("p o a h -> p (o a h)")).then_inc(s_bw, 1)
                act.reg_add(pairs, pairs, 1)

            def copy_b_when_free(w):
                act.wait_ge(s_ex, pairs)
                copy_b(w)

            def body(i):
                win = load_windows(act, i)
                if isinstance(i, int) and i == 0:
                    copy_b(win[0][0])
                for k in steps(i):
                    if there(i, k):
                        further(act, *win[k], copy_b_when_free)
                        if there(i, k + 1):
                            copy_b_when_free(win[k + 1][0])
                        else:
                            act.wait_ge(s_ex, pairs)
                        act.activation(h1[:, k % 2, 0, :], bank[k % 2][:, :], ACT.Relu).then_inc(s_h1h, 1)
                    if there(i, k - 1):
                        act.wait_ge(s_w2, i * U + k)
                        act.activation(h2_hi[:, (k - 1) % 2, :, 0:H],
                                       bank[2 + (k - 1) % 2][:, :].rearrange("p (t h) -> p t h", t=TB),
                                       ACT.Relu).then_inc(s_h2h, 1)
            bodies(act, body)

            act.wait_ge(s_fx, 16 * 9)
            act.copy(f_bias_hi[0:2, :].bitcast(F32R), f_bias_in[0:2, :]).then_inc(s_fbh, 1)

            def final(g, k, half):
                n = size(g, 1)
                if n:
                    act.wait_ge(s_fg, g)
                    if used(g, 1):
                        act.wait_ge(s_fh, g - 2)
                    act.copy(f_msg[:, 1 - k, 0:n * P], bank[4][:, 0:n * P]).then_inc(s_fa, 1)
                n = size(g)
                if n:
                    act.wait_ge(s_fmt, g + 1)
                    if used(g):
                        act.wait_ge(s_fg, g - 1)
                    act.copy(f_feat[:, k, 0, 0:n * P], bank[0][:, 0:n * P]).then_inc(s_fc, 1)
                n = size(g, 2)
                if n:
                    act.wait_ge(s_fh, g - 1)
                    if used(g, 2):
                        act.wait_ge(s_fu, g - 3)
                    for h in range(KH):
                        act.activation(f_hid[:, k, h, 0:n * P], bank[5 + h][:, 0:n * P],
                                       ACT.Relu, bias=bn1_col[:, h:h + 1]).then_inc(s_fhr, 1)
                n = size(g)
                if n:
                    act.copy(f_feat[:, k, 2, 0:n * P], bank[2][:, 0:n * P]).then_inc(s_fcx, 1)
                n = size(g, 4)
                if n:
                    act.wait_ge(s_fe, g - 3)
                    act.activation(f_sd[:, k, 0:n], f_ve[:, k, 0:n], ACT.Sqrt).then_inc(s_fs, 1)
            groups(act, final, 4)

        @block.vector
        def _(dve):
            dve.wait_ge(s_const, 8)
            dve.wait_ge(s_hi, 3)
            dve.tensor_tensor(wab[:, 1, :], w_stage[:, 0:2 * H], wab[:, 0, :].bitcast(F32), ALU.subtract
                              ).then_inc(s_split, 1)
            dve.tensor_tensor(w2[:, 1, :, :].rearrange("p k h -> p (k h)"), w_stage[:, 2 * H:4 * H],
                              w2[:, 0, :, :].rearrange("p k h -> p (k h)").bitcast(F32), ALU.subtract
                              ).then_inc(s_split, 1)
            dve.tensor_tensor(rows_lo[0:2, :, :], rows_in[0:2, :, :], rows_hi[0:2, :, :], ALU.subtract
                              ).then_inc(s_lo, 1)
            dve.wait_ge(s_lo, 1)

            dve.tensor_scalar(rows_hi[0:2, :, :], rows_hi[0:2, :, :], ident[0:2, 0:1], None, ALU.mult
                              ).then_inc(s_lo, 1)
            dve.wait_ge(s_lo, 2)
            for a, rows in enumerate((b1_rows, b2_rows)):
                for j in range(2):
                    dve.scalar_tensor_tensor(rows[:, j * H:(j + 1) * H], rows_lo[0:2, a, :], ident[0:2, 1:2],
                                             rows_hi[0:2, a, :], ALU.mult, ALU.add).then_inc(s_split, 1)
            dve.wait_ge(s_edges, 16 * len(loads))
            dve.tensor_copy(edges_f[0:BG, :], edges_in[0:BG, :]).then_inc(s_ef, 1)
            dve.tensor_copy(edges16[0:BG, :], edges_in[0:BG, 0:GR * EB]).then_inc(s_d16, 1)
            dve.wait_ge(s_ef, 1)
            dst_f = edges_f[0:BG, 0:GR * EB].rearrange("b (g e) -> b g e", g=GR)
            for n, op in enumerate((ALU.min, ALU.max)):
                dve.tensor_reduce(minmax[0:BG, n:2 * GR:2], dst_f, AX.X, op).then_inc(s_mm, 1)
            dve.wait_ge(s_mm, 2)
            dve.tensor_copy(minmax_i[0:BG, :], minmax[0:BG, :]).then_inc(s_wi, 1)
            dve.wait_ge(s_wi, 1)
            dve.tensor_single_scalar(win_i[0:BG, :], minmax_i[0:BG, :], 7, ALU.arith_shift_right
                                     ).then_inc(s_win, 1)
            for n, col in enumerate((dst_col, src_idx)):
                for g in range(GR):
                    dve.wait_ge(s_et, n * GR + g + 1)
                    dve.tensor_copy(col[:, g * BG * TB:(g + 1) * BG * TB].rearrange("p (b t) -> p t b", t=TB),
                                    bank[n * GR + g][:, 0:TB * BG].rearrange("p (t b) -> p t b", t=TB)
                                    ).then_inc(s_ec, 1)

            def tables(g, k, half):
                n = size(g)
                if n:
                    dve.wait_ge(s_xh, g + 1)
                    dve.tensor_tensor(xl[:, k, 0:n * P], bank[k][:, 0:n * P], xh[:, k, 0:n * P].bitcast(F32),
                                      ALU.subtract).then_inc(s_xl, 1)
                n = size(g, 1)
                for q in range((n + 1) // 2):
                    m = min(n - 2 * q, 2)
                    dve.wait_ge(s_bh, g * 2 - 2 + (q + 1))
                    both = b_tab[:, bass.ds(g * GW - GW + 2 * q, m), :, :]
                    dve.tensor_tensor(both[:, :, 1, :], bank[4 + q][:, 0:m * H].rearrange("p (w h) -> p w h", h=H),
                                      both[:, :, 0, :], ALU.subtract).then_inc(s_bl, 1)
            groups(dve, tables, 1)
            dve.wait_ge(s_bl, NPAIR)
            for k in range(2):
                dve.wait_ge(s_as[k], 16 * ((NG + 1 - k) // 2))
            dve.wait_ge(s_row, 16)
            made_t = dve.alloc_register("expanded_pairs_dve")
            made = dve.alloc_register("summed_pairs_dve")
            dve.reg_mov(made_t, 0)
            dve.reg_mov(made, 0)

            def onehot_t_of(k, w):
                at = k % 2 * EB
                dve.tensor_scalar(onehot_t[:, :], dst_all[:, k % U // 2, at:at + EB], node_id[:, bass.ds(w, 1)],
                                  None, ALU.is_equal).then_inc(s_ot, 1)
                dve.reg_add(made_t, made_t, 1)

            def onehot_t_when_free(k, w):
                dve.wait_ge(s_ex, made_t)
                onehot_t_of(k, w)

            def onehot_of(i, k, w):
                for t in range(TB):
                    ins = dve.tensor_scalar(onehot[:, t, :], iota16[:, bass.ds(w * P, P)],
                                            dst_col[:, bass.ds(i * (U * TB) + (k * TB + t), 1)],
                                            None, ALU.is_equal)
                ins.then_inc(s_oh, 1)
                dve.reg_add(made, made, 1)

            def add_sums(w):
                dve.wait_ge(s_sg, made)
                sums = agg[:, bass.ds(w * HC, HC)]
                dve.tensor_tensor(sums, bank[4][:, 0:HC], sums, ALU.add)

            def body(i):
                win = load_windows(dve, i)
                if isinstance(i, int) and i == 0:
                    dve.wait_ge(s_da[0], 16)
                    onehot_t_of(0, win[0][0])
                    dve.memset(agg[:, :], 0.0).then_inc(s_zero, 1)
                    dve.wait_ge(s_zero, 1)
                for k in steps(i):
                    if there(i, k):
                        further(dve, *win[k], lambda w: onehot_t_when_free(k, w))
                        if there(i, k + 1):
                            if (k + 1) % 2 == 0:
                                dve.wait_ge(s_da[(k + 1) % U // 2], i * 16 + 16 * ((k + 1) // U + 1))
                            onehot_t_when_free(k + 1, win[k + 1][0])
                        dve.wait_ge(s_h1h, i * U + (k + 1))
                        dve.scalar_tensor_tensor(h1[:, k % 2, 1, :], bank[k % 2][:, :], 0.0,
                                                 h1[:, k % 2, 0, :].bitcast(F32), ALU.max, ALU.subtract
                                                 ).then_inc(s_h1l, 1)
                    if there(i, k - 1):
                        dve.wait_ge(s_h2h, i * U + k)
                        dve.scalar_tensor_tensor(h2_lo[:, (k - 1) % 2, :, :],
                                                 bank[2 + (k - 1) % 2][:, :].rearrange("p (t h) -> p t h", t=TB),
                                                 0.0, h2_hi[:, (k - 1) % 2, :, 0:H].bitcast(F32),
                                                 ALU.max, ALU.subtract).then_inc(s_h2l, 1)
                    if there(i, k - 2):
                        lo, hi = win[k - 2]
                        with dve.If(lo < hi):
                            with dve.Fori(lo, hi) as w:
                                add_sums(w)
                                onehot_of(i, k - 2, w + 1)
                        add_sums(hi)
                    if there(i, k - 1):
                        onehot_of(i, k - 1, win[k - 1][0])
            bodies(dve, body)
            dve.engine_nop().then_inc(s_end, 1)

            agg3 = agg[:, :].rearrange("p (w c) -> p w c", c=HC)

            def reciprocal_counts(g, k, n):
                dve.tensor_scalar(f_cnt[:, k, 0:n], agg3[:, bass.ds(g * GW, n), H:H + 1]
                                  .rearrange("p w o -> p (w o)"), 1.0, None, ALU.max).then_inc(s_f1, 1)
                dve.wait_ge(s_f1, g + 1)
                dve.reciprocal(f_rec[:, k, 0:n], f_cnt[:, k, 0:n]).then_inc(s_f2, 1)

            def means(g, k, n):
                for j in range(n):
                    ins = dve.tensor_scalar(f_mean[:, k, j, :], agg[:, bass.ds((g * GW + j) * HC, HC)],
                                            f_rec[:, k, j:j + 1], None, ALU.mult)
                ins.then_inc(s_fm, 1)

            reciprocal_counts(0, 0, size(0))
            dve.wait_ge(s_f2, 1)
            means(0, 0, size(0))
            dve.wait_ge(s_fbh, 1)
            dve.tensor_tensor(f_bias_lo[0:2, :], f_bias_in[0:2, :], f_bias_hi[0:2, :], ALU.subtract
                              ).then_inc(s_fbl, 1)
            dve.wait_ge(s_fbl, 1)
            dve.tensor_scalar(f_bias_hi[0:2, :], f_bias_hi[0:2, :], ident[0:2, 0:1], None, ALU.mult
                              ).then_inc(s_fbl, 1)
            dve.wait_ge(s_fbl, 2)
            for to, a in [(b3_rows, 0)] + [(bn2_rows[:, j * D:(j + 1) * D], D) for j in range(GW)]:
                dve.scalar_tensor_tensor(to, f_bias_lo[0:2, a:a + D], ident[0:2, 1:2], f_bias_hi[0:2, a:a + D],
                                         ALU.mult, ALU.add).then_inc(s_fbr, 1)

            def final(g, k, half):
                ahead = size(g, -1)
                if ahead:
                    reciprocal_counts(g + 1, 1 - k, ahead)
                n = size(g, 4)
                if n:
                    dve.wait_ge(s_fu, g - 3)
                    if used(g, 4):
                        dve.wait_ge(s_fo, g - 5)
                    y = f_y[:, k, 0:n * D]
                    dve.scalar_tensor_tensor(y.rearrange("p (w d) -> p w d", d=D),
                                             f_x[:, bass.ds(g * GW - 4 * GW, n), :], 2.0,
                                             bank[7][:, 0:n * D].rearrange("p (w d) -> p w d", d=D),
                                             ALU.mult, ALU.add).then_inc(s_fy, 1)
                    dve.wait_ge(s_fy, g - 3)
                    for j in range(n):
                        dve.bn_stats(f_bn[:, k, j, :], y[:, j * D:(j + 1) * D]).then_inc(s_fn, 1)
                    if n < GW or isinstance(g, int):
                        dve.wait_ge(s_fn, GW * (g - 4) + n)
                    else:
                        dve.wait_ge(s_fn, g * GW - 3 * GW)
                if ahead:
                    dve.wait_ge(s_f2, g + 2)
                    if used(g, -1):
                        dve.wait_ge(s_fmt, g)
                    means(g + 1, 1 - k, ahead)
                if n:
                    for j in range(n):
                        dve.bn_aggr(f_mv[:, k, j, :], f_bn[:, k, j, :]).then_inc(s_fv, 1)
                    if n < GW or isinstance(g, int):
                        dve.wait_ge(s_fv, GW * (g - 4) + n)
                    else:
                        dve.wait_ge(s_fv, g * GW - 3 * GW)
                    dve.tensor_scalar(f_ve[:, k, 0:n], f_mv[:, k, 0:n, 1:2].rearrange("p w o -> p (w o)"),
                                      EPS, None, ALU.add).then_inc(s_fe, 1)
                n = size(g)
                if n:
                    dve.wait_ge(s_fmt, g + 1)
                    if used(g):
                        dve.wait_ge(s_fg, g - 1)
                    dve.tensor_copy(f_feat[:, k, 1, 0:n * P], bank[1][:, 0:n * P])
                    dve.tensor_copy(f_row[k][:, 0:n * P], bank[3][0:2, 0:n * P]).then_inc(s_fr, 1)
                n = size(g, 5)
                if n:
                    j = 1 - k
                    dve.wait_ge(s_fs, g - 4)
                    dve.reciprocal(f_rs[:, j, 0:n], f_sd[:, j, 0:n]).then_inc(s_fq, 1)
                    dve.wait_ge(s_fq, g - 4)
                    if used(g, 5):
                        dve.wait_ge(s_fst[j], ((g - 5) // 2 if isinstance(g, int) else half - 3 + k) * 16)
                    for w in range(n):
                        ins = dve.tensor_scalar(f_out[:, j, w, :], f_y[:, j, w * D:(w + 1) * D],
                                                f_mv[:, j, w, 0:1], f_rs[:, j, w:w + 1], ALU.subtract, ALU.mult)
                    ins.then_inc(s_fo, 1)
            dve.wait_ge(s_fx, 16 * 9)
            groups(dve, final, 5, 1)

        @block.tensor
        def _(pe):
            pe.wait_ge(s_const, 8)
            pe.wait_ge(s_ef, 1)
            for n in range(2):
                for g in range(GR):
                    for t in range(TB):
                        at = (n * GR + g) * EB + t * P
                        ins = pe.transpose(bank[n * GR + g][:, t * BG:(t + 1) * BG], edges_f[0:BG, at:at + P],
                                           ident[0:BG, 0:BG])
                    ins.then_inc(s_et, 1)
            pe.wait_ge(s_ec, 2 * GR)
            pe.wait_ge(s_split, 6)

            def tables(g, k, half):
                n = size(g)
                if n:
                    extra = 1 if n < GW and n > 1 else 0
                    pe.wait_ge(s_xs[k], 16 * (half + 1 + extra))
                    if used(g):
                        pe.wait_ge(s_xl, g - 1)
                    for j in range(n):
                        ins = pe.transpose(bank[k][:, j * P:(j + 1) * P], x_slot[:, k, j, :], ident[:, :])
                    ins.then_inc(s_xt, 1)
                n = size(g, 1)
                if n:
                    pe.wait_ge(s_xl, g)
                for q in range((n + 1) // 2):
                    m = min(n - 2 * q, 2)
                    if used(g, 0):
                        pe.wait_ge(s_ac, g * 2 - 4 + (q + 1))
                        pe.wait_ge(s_bl, g * 2 - 4 + (q + 1))
                    pe.matmul(bank[4 + q][:, 0:m * H], ones2[:, :], b1_rows[:, 0:m * H], start=True, stop=False,
                              skip_group_check=True)
                    for w in range(m):
                        v = slice((2 * q + w) * P, (2 * q + w + 1) * P)
                        for c in range(2):
                            for n_, (xp, a) in enumerate(((xh, 0), (xh, 1), (xl, 0))):
                                ins = pe.matmul(bank[2 + 2 * c + q][:, w * H:(w + 1) * H], xp[:, 1 - k, v],
                                                wab[:, a, c * H:(c + 1) * H],
                                                start=(c == 0 and w == 0 and n_ == 0), stop=(n_ == 2),
                                                skip_group_check=True)
                    ins.then_inc(s_ab, 1)
            groups(pe, tables, 1)
            pe.wait_ge(s_row, 16)
            pe.wait_ge(s_ac, NPAIR)
            pe.wait_ge(s_bl, NPAIR)
            expanded = pe.alloc_register("expanded_pairs_pe")
            summed = pe.alloc_register("summed_pairs_pe")
            pe.reg_mov(expanded, 0)
            pe.reg_mov(summed, 0)

            def expand(k, last=False):
                pe.reg_add(expanded, expanded, 1)
                pe.wait_ge(s_ot, expanded)
                pe.wait_ge(s_bw, expanded)
                for h in range(KH):
                    for a in range(2):
                        ins = pe.matmul(bank[k % 2][:, h * EB:(h + 1) * EB], b_win[:, a, h * P:(h + 1) * P],
                                        onehot_t[:, :], start=False, stop=True, skip_group_check=True)
                ins.then_inc(s_ex, 1)

            def sum_segments(k):
                pe.reg_add(summed, summed, 1)
                pe.wait_ge(s_oh, summed)
                for t in range(TB):
                    pe.matmul(bank[4][:, 0:HC], onehot[:, t, :], h2_hi[:, k % 2, t, :], start=(t == 0),
                              stop=False, skip_group_check=True)
                    ins = pe.matmul(bank[4][:, 0:H], onehot[:, t, :], h2_lo[:, k % 2, t, :], start=False,
                                    stop=(t == TB - 1), skip_group_check=True)
                ins.then_inc(s_sg, 1)

            def body(i):
                win = load_windows(pe, i)
                for k in steps(i):
                    if there(i, k):
                        for t in range(TB):
                            pe.wait_ge(s_g[k * TB + t], i * 16 + 16)
                            for h in range(KH):
                                ins = pe.matmul(bank[k % 2][:, h * EB + t * P:h * EB + (t + 1) * P],
                                                a_edge[:, k * TB + t, h * P:(h + 1) * P], ident[:, :],
                                                start=(t == 0 and h == 0), stop=False, is_transpose=True,
                                                skip_group_check=True)
                        ins.then_inc(s_ta, 1)
                        expand(k)
                        further(pe, *win[k], lambda w: expand(k))
                    if there(i, k - 1):
                        j = (k - 1) % 2
                        pe.wait_ge(s_h1l, i * U + k)
                        pe.matmul(bank[2 + j][:, :], ones2[:, :], b2_rows[:, :], start=True, stop=False,
                                  skip_group_check=True)
                        for t in range(TB):
                            to = bank[2 + j][:, t * H:(t + 1) * H]
                            for a, b in ((0, 0), (0, 1), (1, 0)):
                                for h in range(KH):
                                    ins = pe.matmul(to, h1[:, j, a, h * EB + t * P:h * EB + (t + 1) * P],
                                                    w2[:, b, h, :], start=False, stop=(a == 1 and h == KH - 1),
                                                    skip_group_check=True)
                        ins.then_inc(s_w2, 1)
                    if there(i, k - 2):
                        pe.wait_ge(s_h2l, i * U + (k - 1))
                        sum_segments(k - 2)
                        further(pe, *win[k - 2], lambda w: sum_segments(k - 2))
            bodies(pe, body)
            pe.wait_ge(s_fx, 16 * 9)
            pe.wait_ge(s_fbr, 1 + GW)

            def final(g, k, half):
                n = size(g)
                if n:
                    pe.wait_ge(s_fm, g + 1)
                    pe.wait_ge(s_fxs, g + 1)
                    if not isinstance(g, int) or g >= 1:
                        pe.wait_ge(s_fcx, g)
                        pe.wait_ge(s_fr, g)
                    for w in range(n):
                        v = slice(w * P, (w + 1) * P)
                        for h in range(KH):
                            pe.transpose(bank[h][:, v], f_mean[:, k, w, h * P:(h + 1) * P], ident[:, :])
                        pe.transpose(bank[2][:, v], f_xs[:, k, w, :], ident[:, :])
                        ins = pe.transpose(bank[3][0:2, v], f_mean[:, k, w, H:HC], ident[:, :])
                    ins.then_inc(s_fmt, 1)
                j = 1 - k
                n = size(g, 1) * P
                if n:
                    pe.wait_ge(s_fc, g)
                    pe.wait_ge(s_fr, g)
                    if used(g):
                        pe.wait_ge(s_fa, g - 1)
                    for h in range(KH):
                        pe.matmul(bank[4][:, 0:n], w3[:, h, :], f_feat[:, j, h, 0:n], start=(h == 0), stop=False)
                    pe.matmul(bank[4][:, 0:n], b3_rows, f_row[j][:, 0:n], start=False, stop=True
                              ).then_inc(s_fg, 1)
                n = size(g, 2) * P
                if n:
                    pe.wait_ge(s_fa, g - 1)
                    pe.wait_ge(s_fcx, g - 1)
                    if used(g, 1):
                        pe.wait_ge(s_fhr, g * 2 - 4)
                    for h in range(KH):
                        to = bank[5 + h][:, 0:n]
                        pe.matmul(to, wn1[:, 0, h * P:(h + 1) * P], f_feat[:, k, 2, 0:n], start=True, stop=False)
                        ins = pe.matmul(to, wn1[:, 1, h * P:(h + 1) * P], f_msg[:, k, 0:n], start=False, stop=True)
                    ins.then_inc(s_fh, 1)
                n = size(g, 3)
                if n:
                    pe.wait_ge(s_fhr, g * 2 - 4)
                    if used(g, 2):
                        pe.wait_ge(s_fy, g - 3)
                    pe.matmul(bank[7][:, 0:n * D], ones2[:, :], bn2_rows[:, 0:n * D], start=True, stop=False,
                              skip_group_check=True)
                    for w in range(n):
                        for h in range(KH):
                            ins = pe.matmul(bank[7][:, w * D:(w + 1) * D], f_hid[:, j, h, w * P:(w + 1) * P],
                                            wn2[:, h, :], start=False, stop=(h == KH - 1), skip_group_check=True)
                    ins.then_inc(s_fu, 1)
            groups(pe, final, 3)


_INS = ["x", "src", "dst"] + ["L0_gnn_" + n for n in
                              ("Wm1", "bm1", "Wm2", "bm2", "Wm3", "bm3", "Wn1", "bn1", "Wn2", "bn2")]


def kernel(**inputs):
    import numpy as np
    import concourse.bacc as bacc
    from concourse.bass_utils import run_bass_kernel_spmd

    nc = bacc.Bacc("TRN2", target_bir_lowering=False, num_devices=1)
    arrays, args = {}, []
    for name in _INS:
        a = np.ascontiguousarray(inputs[name])
        arrays[f"in_{name}"] = a
        args.append(nc.dram_tensor(f"in_{name}", a.shape, mybir.dt.from_np(a.dtype), kind="ExternalInput").ap())
    shape = inputs["x"].shape
    args.append(nc.dram_tensor("out_0", shape, F32, kind="ExternalOutput").ap())
    gnn_layer(nc, *args)
    r = run_bass_kernel_spmd(nc, [arrays], core_ids=[0])
    return r.results[0]["out_0"]
```

```python
from contextlib import ExitStack

import numpy as np

import concourse.bass as bass
from concourse import mybir

F32 = mybir.dt.float32
F32R = mybir.dt.float32r
I32 = mybir.dt.int32
I16 = mybir.dt.int16
ALU = mybir.AluOpType
ACT = mybir.ActivationFunctionType
AX = mybir.AxisListType

P = 128
TB = 2
EB = TB * P
U = 4
EPS = 1e-5


def gnn_layer(nc, x, src, dst, Wm1, bm1, Wm2, bm2, Wm3, bm3, Wn1, bn1, Wn2, bn2, out):
    N, D = x.shape
    (E,) = src.shape
    H = Wm1.shape[1]
    KH = H // P
    NW = -(-N // P)
    NLAST = N - (NW - 1) * P
    NB = -(-E // EB)
    NB = -(-NB // U) * U
    GR = 4
    BG = NB // GR
    NI = NB // U
    PAD_DST = NW * P - 1
    GW = 4
    NG = -(-NW // GW)
    HC = H + 2
    assert D == P and H == 2 * P and BG <= P and NI >= 3 and NW >= 4 and NW * P > N

    a_table = nc.dram_tensor("a_table", [NW * P, H], F32, kind="Internal").ap()
    dst16_dram = nc.dram_tensor("dst16_dram", [NB, EB], I16, kind="Internal").ap()
    win_dram = nc.dram_tensor("win_dram", [NB, 2], I32, kind="Internal").ap()

    with ExitStack() as ctx:
        def sb(name, shape, dt):
            return ctx.enter_context(nc.sbuf_tensor(name, shape, dt))

        def sem(name):
            return ctx.enter_context(nc.semaphore(name))

        b_tab = sb("b_tab", [P, NW, 2, H], F32)
        agg = sb("agg", [P, NW * HC], F32)
        iota16 = sb("iota16", [P, P], I16)
        first_node = sb("first_node", [P, NW], F32)
        node_id = sb("node_id", [P, NW], F32)
        src_idx = sb("src_idx", [P, NB * TB], I32)
        dst_col = sb("dst_col", [P, NB * TB], F32)
        win_row = sb("win_row", [1, 2 * (NB + 8)], I32)
        w2 = sb("w2", [P, 2, KH, H], F32R)
        b2_rows = sb("b2_rows", [2, 2 * H], F32R)
        ones2 = sb("ones2", [2, P], F32R)
        ident = sb("ident", [P, P], F32)
        a_edge = sb("a_edge", [P, U * TB, H], F32)
        idx_now = sb("idx_now", [P, U * TB], I32)
        zero_idx = sb("zero_idx", [P, TB], I32)
        dst_all = sb("dst_all", [P, 2, 2 * EB], I16)
        onehot_t = sb("onehot_t", [P, 2, EB], F32R)
        b_win = sb("b_win", [P, 2, 2, H], F32R)
        onehot = sb("onehot", [P, 2, TB, P], F32R)
        h1 = sb("h1", [P, 2, 2, KH * EB], F32R)
        h2_hi = sb("h2_hi", [P, 2, TB, HC], F32R)
        h2_lo = sb("h2_lo", [P, 2, TB, H], F32R)

        bank = [ctx.enter_context(nc.psum_tensor(f"bank{i}", [P, 512], F32)) for i in range(8)]

        wab = h1[:, 0, :, :]
        xl = h1[:, 1, :, :]
        xh = h2_lo[:, :, :, :].rearrange("p s t h -> p s (t h)")
        b1_rows = b_win[0:2, 0, :, :].rearrange("p a h -> p (a h)")
        edges_in = a_edge[:, :, :].rearrange("p a h -> p (a h)").bitcast(I32)

        class Carve:
            def __init__(self, region, limit):
                self.region, self.at, self.limit = region, 0, limit

            def __call__(self, *shape):
                cols = int(np.prod(shape))
                v = self.region[:, self.at:self.at + cols]
                self.at += cols
                assert self.at <= self.limit
                if len(shape) == 2:
                    return v.rearrange("p (a b) -> p a b", a=shape[0])
                if len(shape) == 3:
                    return v.rearrange("p (a b c) -> p a b c", a=shape[0], b=shape[1])
                return v

        carve = Carve(agg, NW * HC)
        w_stage = carve(4 * H)
        x_slot = carve(2, GW, D)
        a_out = carve(2, GW, H)
        edges_f = carve(2 * GR * EB)
        edges16 = carve(GR * EB // 2).bitcast(I16)
        rows_in = carve(2, H)
        rows_hi = carve(2, H)
        rows_lo = carve(2, H)
        minmax = carve(2 * GR)
        minmax_i = carve(2 * GR).bitcast(I32)
        win_i = carve(2 * GR).bitcast(I32)
        carve = Carve(b_tab[:, :, :, :].rearrange("p w a h -> p (w a h)"), NW * 2 * H)
        f_x = carve(NW, D)
        f_xs = carve(2, GW, D)
        f_cnt, f_rec = carve(2, GW), carve(2, GW)
        f_mean = carve(2, GW, HC)
        f_feat = carve(2, 3, GW * P)
        f_msg = carve(2, GW * P)
        f_hid = carve(2, KH, GW * P)
        f_y, f_out = carve(2, GW * D), carve(2, GW, D)
        f_bn, f_mv = carve(2, GW, 6), carve(2, GW, 2)
        f_ve, f_sd, f_rs = carve(2, GW), carve(2, GW), carve(2, GW)
        w3, wn1, wn2 = carve(KH, D), carve(2, H), carve(KH, D)
        bn1_col = carve(KH)
        f_bias_in, f_bias_hi, f_bias_lo = carve(2 * D), carve(2 * D), carve(2 * D)
        f_row = [h1[0:2, k, 0, :] for k in range(2)]
        bn2_rows = h1[0:2, 0, 1, :]
        b3_rows = h1[0:2, 1, 1, 0:D]

        s_w = sem("s_weights_loaded")
        s_edges = sem("s_edges_loaded")
        s_pad = sem("s_padding_set")
        s_zeros = sem("s_ident_zeroed")
        s_const = sem("s_constants")
        s_hi = sem("s_weights_hi")
        s_lo = sem("s_bias_parts")
        s_split = sem("s_weights_split")
        s_ef = sem("s_edges_as_float")
        s_mm = sem("s_min_max")
        s_wi = sem("s_min_max_int")
        s_win = sem("s_windows_found")
        s_d16 = sem("s_dst16_made")
        s_scr = sem("s_scratch_stored")
        s_row = sem("s_win_row_loaded")
        s_et = sem("s_edges_transposed")
        s_ec = sem("s_edge_columns")
        s_xs = [sem(f"s_x_in_slot{k}") for k in range(2)]
        s_xz = sem("s_last_x_zeroed")
        s_xt = sem("s_x_transposed")
        s_xh = sem("s_x_hi")
        s_xl = sem("s_x_lo")
        s_ab = sem("s_ab_product")
        s_ac = sem("s_a_copied")
        s_as = [sem(f"s_a_stored{k}") for k in range(2)]
        s_bh = sem("s_b_hi")
        s_bl = sem("s_b_lo")
        s_zero = sem("s_agg_zeroed")
        s_idx = sem("s_idx_copied")
        s_g = [sem(f"s_gathered{t}") for t in range(U * TB)]
        s_da = [sem(f"s_dst_all{c}") for c in range(2)]
        s_ta = sem("s_a_transposed")
        s_ot = [sem(f"s_onehot_t_made{k}") for k in range(2)]
        s_bw = [sem(f"s_b_win_copied{k}") for k in range(2)]
        s_ex = [sem(f"s_expanded{k}") for k in range(2)]
        s_h1h = sem("s_h1_hi")
        s_h1l = sem("s_h1_lo")
        s_w2 = sem("s_h2_product")
        s_h2h = sem("s_h2_hi")
        s_h2l = sem("s_h2_lo")
        s_oh = [sem(f"s_onehot_made{k}") for k in range(2)]
        s_sg = [sem(f"s_segments_summed{k}") for k in range(2)]
        s_end = sem("s_sums_complete")
        s_fz = sem("s_final_x_zeroed")
        s_fx = sem("s_final_loaded")
        s_f1 = sem("s_count_clamped")
        s_f2 = sem("s_count_inverted")
        s_fm = sem("s_mean")
        s_fxs = sem("s_final_x_in_slot")
        s_fbh = sem("s_final_bias_hi")
        s_fbl = sem("s_final_bias_lo")
        s_fbr = sem("s_final_bias_rows")
        s_fmt = sem("s_mean_transposed")
        s_fc = sem("s_features_copied")
        s_fcx = sem("s_final_x_copied")
        s_fr = sem("s_mask_row")
        s_fg = sem("s_message_product")
        s_fa = sem("s_message_copied")
        s_fh = sem("s_hidden_product")
        s_fhr = sem("s_hidden_relu")
        s_fu = sem("s_update_product")
        s_fy = sem("s_residual_added")
        s_fn = sem("s_bn_stats")
        s_fv = sem("s_mean_variance")
        s_fe = sem("s_variance_eps")
        s_fs = sem("s_std")
        s_fq = sem("s_std_inverted")
        s_fo = sem("s_normalised")
        s_fst = [sem(f"s_out_stored{k}") for k in range(2)]

        def groups(e, step, lag, ahead=0):
            first = lag + 2
            count = (NG - 1 - ahead - first) // 2
            for g in range(first):
                step(g, g % 2, g // 2)
            with e.Fori(0, count) as i:
                for k in range(2):
                    step(i * 2 + (first + k), (first + k) % 2, i + (first + k) // 2)
            for g in range(first + 2 * count, NG + lag):
                step(g, g % 2, g // 2)

        def size(g, back=0):
            if isinstance(g, int) and not 0 <= g - back < NG:
                return 0
            return NW - (NG - 1) * GW if isinstance(g, int) and g - back == NG - 1 else GW

        def used(g, back=0):
            return not isinstance(g, int) or g - back >= 2

        def load_x(e, g, n, to, done):
            whole = n if not (isinstance(g, int) and g == NG - 1) else n - 1
            if whole:
                e.dma_start(to[:, 0:whole, :], x[bass.ds(g * (GW * P), whole * P), :]
                            .rearrange("(w p) d -> p w d", p=P)).then_inc(done, 16)
            if whole < n:
                e.dma_start(to[0:NLAST, whole, :], x[N - NLAST:N, :]).then_inc(done, 16)

        def bodies(e, body):
            body(0)
            with e.Fori(1, NI - 1) as i:
                body(i)
            body(NI - 1)

        def there(i, k):
            return not isinstance(i, int) or 0 <= U * i + k < NB

        def load_windows(e, i):
            vals = nc.values_load_multi_w_load_instructions(
                win_row[0:1, bass.ds(i * (2 * U), 2 * (U + 4))], engines=[e.engine], min_val=0, max_val=NW - 1,
                skip_runtime_bounds_check_because="dst is a node's number")[1]
            return {k: (vals[2 * k + 4], vals[2 * k + 5]) for k in range(-2, U + 2)}

        def further(e, lo, hi, step):
            with e.If(lo < hi):
                with e.Fori(lo + 1, hi + 1) as w:
                    step(w)

        def after(lo):
            return nc.s_assert_within(lo + 1, 1, NW - 1, skip_runtime_bounds_check_because="lo < hi")

        def steps(i):
            return range(U + 2) if isinstance(i, int) and i == NI - 1 else range(U)

        full = E // EB
        assert (GR - 1) * BG <= full
        loads = []
        for n in range(2):
            for g in range(GR):
                rows = min(full - g * BG, BG)
                if rows:
                    loads.append((n, g, 0, rows, EB))
            if E % EB:
                loads.append((n, GR - 1, rows, 1, E % EB))

        NPAIR = 2 * (NG - 1) + (size(NG - 1) + 1) // 2

        block = ctx.enter_context(nc.Block())

        @block.sync
        def _(sp):
            sp.wait_ge(s_pad, 2)
            for n, g, row, rows, edges in loads:
                at, e0 = (n * GR + g) * EB, (g * BG + row) * EB
                sp.dma_start(edges_in[row:row + rows, at:at + edges],
                             (dst, src)[n][e0:e0 + rows * edges].rearrange("(b e) -> b e", e=edges)
                             ).then_inc(s_edges, 16)
            for g in range(2):
                load_x(sp, g, GW, x_slot[:, g, :, :], s_xs[g])
            sp.wait_ge(s_win, 1)
            sp.wait_ge(s_d16, 1)
            for g in range(GR):
                sp.dma_start(win_dram[g * BG:(g + 1) * BG, :], win_i[0:BG, 2 * g:2 * g + 2]).then_inc(s_scr, 16)
                sp.dma_start(dst16_dram[g * BG:(g + 1) * BG, :],
                             edges16[0:BG, g * EB:(g + 1) * EB]).then_inc(s_scr, 16)
            sp.wait_ge(s_scr, 32 * GR)
            sp.dma_start(win_row[0:1, 4:4 + 2 * NB], win_dram.rearrange("(o b) c -> o (b c)", o=1)
                         ).then_inc(s_row, 16)

            def tables(g, k, half):
                if size(g) and used(g):
                    sp.wait_ge(s_xt, g - 1)
                    if size(g) < GW:
                        sp.wait_ge(s_xz, 1)
                    load_x(sp, g, size(g), x_slot[:, k, :, :], s_xs[k])
                n = size(g, 2)
                if n:
                    sp.wait_ge(s_ac, g * 2 - 2 if n > 2 else g * 2 - 3)
                    sp.dma_start(a_table[bass.ds((g - 2) * (GW * P), n * P), :]
                                 .rearrange("(w p) h -> p w h", p=P), a_out[:, k, 0:n, :]).then_inc(s_as[k], 16)
            groups(sp, tables, 2)

            def body(i):
                for c in range(2):
                    if there(i, -1):
                        sp.wait_ge(s_h1l, i * U + (2 * c - 2))
                    sp.dma_start(dst_all[:, c, :].rearrange("p (b e) -> p b e", b=2),
                                 dst16_dram[bass.ds(i * U + 2 * c, 2), :].partition_broadcast(P)
                                 ).then_inc(s_da[c], 16)
            bodies(sp, body)

            sp.wait_ge(s_end, 1)
            sp.dma_start(f_x[:, 0:NW - 1, :], x[0:(NW - 1) * P, :].rearrange("(w p) d -> p w d", p=P)
                         ).then_inc(s_fx, 16)
            sp.dma_start(w3, Wm3.rearrange("(k p) d -> p k d", p=P)).then_inc(s_fx, 16)
            sp.dma_start(wn1, Wn1.rearrange("(k p) d -> p k d", p=P)).then_inc(s_fx, 16)
            sp.dma_start(wn2, Wn2.rearrange("(k p) d -> p k d", p=P)).then_inc(s_fx, 16)
            sp.dma_start(f_bias_in[0:2, 0:D], bm3.partition_broadcast(2)).then_inc(s_fx, 16)
            sp.dma_start(f_bias_in[0:2, D:2 * D], bn2.partition_broadcast(2)).then_inc(s_fx, 16)
            for k in range(KH):
                sp.dma_start(bn1_col[:, k:k + 1], bn1[k * P:(k + 1) * P].rearrange("(p o) -> p o", o=1)
                             ).then_inc(s_fx, 16)
            sp.wait_ge(s_fz, 1)
            sp.dma_start(f_x[0:NLAST, NW - 1, :], x[(NW - 1) * P:N, :]).then_inc(s_fx, 16)

            def store_out(g, k, half):
                n = size(g)
                sp.wait_ge(s_fo, g + 1)
                whole = n - 1 if isinstance(g, int) and g == NG - 1 else n
                if whole:
                    sp.dma_start(out[bass.ds(g * (GW * P), whole * P), :].rearrange("(w p) d -> p w d", p=P),
                                 f_out[:, k, 0:whole, :]).then_inc(s_fst[k], 16)
                if whole < n:
                    sp.dma_start(out[N - NLAST:N, :], f_out[0:NLAST, k, whole, :]).then_inc(s_fst[k], 16)
            groups(sp, store_out, 0)
            last = (NG - 1) % 2
            for k in range(2):
                sp.wait_ge(s_fst[k], 16 * ((NG + 1 - k) // 2 + (k == last and size(NG - 1) > 1)))

        @block.gpsimd
        def _(pool):
            pool.memset(edges_in[:, (GR - 1) * EB:GR * EB], PAD_DST).then_inc(s_pad, 1)
            pool.memset(edges_in[:, (2 * GR - 1) * EB:2 * GR * EB], 0).then_inc(s_pad, 1)
            pool.memset(ident[:, :], 0.0).then_inc(s_zeros, 1)
            pool.wait_ge(s_zeros, 1)
            pool.affine_select(out=ident[:, :], in_=ident[:, :], compare_op=ALU.not_equal, fill=1.0,
                               base=0, pattern=[[-1, P]], channel_multiplier=1).then_inc(s_const, 1)
            pool.memset(ones2[:, :].bitcast(F32), 1.0).then_inc(s_const, 1)
            pool.memset(zero_idx[:, :], 0).then_inc(s_const, 1)
            pool.memset(h2_hi[:, :, :, H:HC].bitcast(F32), 1.0).then_inc(s_const, 1)
            pool.iota(node_id[:, :], pattern=[[P, NW]], base=0, channel_multiplier=1,
                      allow_small_or_imprecise_dtypes=True).then_inc(s_const, 1)
            pool.iota(first_node[:, :], pattern=[[P, NW]], base=0, channel_multiplier=0,
                      allow_small_or_imprecise_dtypes=True).then_inc(s_const, 1)
            pool.iota(iota16[:, :], pattern=[[1, P]], base=0, channel_multiplier=0,
                      allow_small_or_imprecise_dtypes=True).then_inc(s_const, 1)
            pool.memset(win_row[0:1, 0:4], 0).then_inc(s_const, 1)
            pool.memset(win_row[0:1, 4 + 2 * NB:2 * (NB + 8)], 0).then_inc(s_const, 1)

            pool.wait_ge(s_xt, NG - 2)
            pool.memset(x_slot[:, (NG - 1) % 2, size(NG - 1) - 1, :], 0.0).then_inc(s_xz, 1)
            for k in range(2):
                pool.wait_ge(s_as[k], 16 * ((NG + 1 - k) // 2))
            pool.wait_ge(s_ec, 2 * GR)

            copied = pool.alloc_register("blocks_with_indices")
            pool.reg_mov(copied, 1)

            def copy_idx(i, k):
                at = k % U * TB
                v = src_idx[:, bass.ds(i * (U * TB) + k * TB, TB)]
                pool.tensor_tensor(idx_now[:, at:at + TB], v, zero_idx[:, :], ALU.add).then_inc(s_idx, 1)

            copy_idx(0, 0)

            def body(i):
                for k in range(U):
                    if there(i, k - U):
                        pool.wait_ge(s_ta, i * U + (k - U + 1))
                    if there(i, k + 1 - U):
                        for t in range(TB):
                            pool.wait_ge(s_g[(k + 1) % U * TB + t], i * 16 + 16 * ((k + 1) // U))
                    if there(i, k + 1):
                        pool.wait_ge(s_idx, copied)
                        copy_idx(i, k + 1)
                    else:
                        pool.wait_ge(s_idx, NB)
                    pool.reg_add(copied, copied, 1)
                    for t in range(k * TB, (k + 1) * TB):
                        pool.indirect_dma_start(a_edge[:, t, :], None, a_table,
                                                bass.IndirectOffsetOnAxis(ap=idx_now[:, t:t + 1], axis=0)
                                                ).then_inc(s_g[t], 16)
            bodies(pool, body)
            pool.wait_ge(s_end, 1)
            pool.memset(f_x[:, NW - 1, :], 0.0).then_inc(s_fz, 1)
            pool.wait_ge(s_fx, 16 * 9)

            def final(g, k, half):
                if used(g):
                    pool.wait_ge(s_fmt, g - 1)
                n = size(g)
                pool.tensor_copy(f_xs[:, k, 0:n, :], f_x[:, bass.ds(g * GW, n), :]).then_inc(s_fxs, 1)
            groups(pool, final, 0)

        @block.scalar
        def _(act):
            act.dma_start(w_stage[:, 0:2 * H].rearrange("p (k h) -> p k h", k=2),
                          Wm1.rearrange("(k p) h -> p k h", p=P)).then_inc(s_w, 16)
            act.dma_start(w_stage[:, 2 * H:4 * H].rearrange("p (k h) -> p k h", k=2),
                          Wm2.rearrange("(k p) h -> p k h", p=P)).then_inc(s_w, 16)
            act.dma_start(rows_in[0:2, 0, :], bm1.partition_broadcast(2)).then_inc(s_w, 16)
            act.dma_start(rows_in[0:2, 1, :], bm2.partition_broadcast(2)).then_inc(s_w, 16)
            act.wait_ge(s_w, 64)
            act.copy(wab[:, 0, :], w_stage[:, 0:2 * H]).then_inc(s_hi, 1)
            act.copy(w2[:, 0, :, :].rearrange("p k h -> p (k h)"), w_stage[:, 2 * H:4 * H]).then_inc(s_hi, 1)
            act.copy(rows_hi[0:2, :, :].bitcast(F32R), rows_in[0:2, :, :]).then_inc(s_hi, 1)

            def tables(g, k, half):
                n = size(g)
                if n:
                    act.wait_ge(s_xt, g + 1)
                    if used(g):
                        act.wait_ge(s_ab, g * 2 - 2)
                    act.copy(xh[:, k, 0:n * P], bank[k][:, 0:n * P]).then_inc(s_xh, 1)
                n = size(g, 1)
                for q in range((n + 1) // 2):
                    m = min(n - 2 * q, 2)
                    act.wait_ge(s_ab, g * 2 - 2 + (q + 1))
                    if used(g, 1) and q == 0:
                        act.wait_ge(s_as[1 - k], ((g - 1) // 2 if isinstance(g, int) else half - 1 + k) * 16)
                    act.copy(a_out[:, 1 - k, 2 * q:2 * q + m, :],
                             bank[2 + q][:, 0:m * H].rearrange("p (w h) -> p w h", h=H)).then_inc(s_ac, 1)
                    act.copy(b_tab[:, bass.ds(g * GW - GW + 2 * q, m), 0, :].bitcast(F32R),
                             bank[4 + q][:, 0:m * H].rearrange("p (w h) -> p w h", h=H)).then_inc(s_bh, 1)
            groups(act, tables, 1)
            act.wait_ge(s_bl, NPAIR)
            act.wait_ge(s_row, 16)
            more = act.alloc_register("further_pairs_act")
            act.reg_mov(more, 1)

            def copy_b(slot, w):
                act.copy(b_win[:, slot, :, :].rearrange("p a h -> p (a h)"),
                         b_tab[:, bass.ds(w, 1), :, :].rearrange("p o a h -> p (o a h)")).then_inc(s_bw[slot], 1)

            def copy_second_b(lo, hi):
                with act.If(lo < hi):
                    act.reg_add(more, more, 1)
                    copy_b(1, after(lo))

            def body(i):
                win = load_windows(act, i)
                if isinstance(i, int) and i == 0:
                    copy_b(0, win[0][0])
                    copy_second_b(*win[0])
                for k in steps(i):
                    if there(i, k):
                        lo, hi = win[k]
                        with act.If(lo + 1 < hi):
                            with act.Fori(lo + 2, hi + 1) as w:
                                act.wait_ge(s_ex[1], more)
                                act.reg_add(more, more, 1)
                                copy_b(1, w)
                        act.wait_ge(s_ex[0], i * U + (k + 1))
                        if there(i, k + 1):
                            copy_b(0, win[k + 1][0])
                        act.wait_ge(s_ex[1], more)
                        act.activation(h1[:, k % 2, 0, :], bank[k % 2][:, :], ACT.Relu).then_inc(s_h1h, 1)
                        if there(i, k + 1):
                            copy_second_b(*win[k + 1])
                    if there(i, k - 1):
                        act.wait_ge(s_w2, i * U + k)
                        act.activation(h2_hi[:, (k - 1) % 2, :, 0:H],
                                       bank[2 + (k - 1) % 2][:, :].rearrange("p (t h) -> p t h", t=TB),
                                       ACT.Relu).then_inc(s_h2h, 1)
            bodies(act, body)

            act.wait_ge(s_fx, 16 * 9)
            act.copy(f_bias_hi[0:2, :].bitcast(F32R), f_bias_in[0:2, :]).then_inc(s_fbh, 1)

            def final(g, k, half):
                n = size(g, 1)
                if n:
                    act.wait_ge(s_fg, g)
                    if used(g, 1):
                        act.wait_ge(s_fh, g - 2)
                    act.copy(f_msg[:, 1 - k, 0:n * P], bank[4][:, 0:n * P]).then_inc(s_fa, 1)
                n = size(g)
                if n:
                    act.wait_ge(s_fmt, g + 1)
                    if used(g):
                        act.wait_ge(s_fg, g - 1)
                    act.copy(f_feat[:, k, 0, 0:n * P], bank[0][:, 0:n * P]).then_inc(s_fc, 1)
                n = size(g, 2)
                if n:
                    act.wait_ge(s_fh, g - 1)
                    if used(g, 2):
                        act.wait_ge(s_fu, g - 3)
                    for h in range(KH):
                        act.activation(f_hid[:, k, h, 0:n * P], bank[5 + h][:, 0:n * P],
                                       ACT.Relu, bias=bn1_col[:, h:h + 1]).then_inc(s_fhr, 1)
                n = size(g)
                if n:
                    act.copy(f_feat[:, k, 2, 0:n * P], bank[2][:, 0:n * P]).then_inc(s_fcx, 1)
                n = size(g, 4)
                if n:
                    act.wait_ge(s_fe, g - 3)
                    act.activation(f_sd[:, k, 0:n], f_ve[:, k, 0:n], ACT.Sqrt).then_inc(s_fs, 1)
            groups(act, final, 4)

        @block.vector
        def _(dve):
            dve.wait_ge(s_const, 9)
            dve.wait_ge(s_hi, 3)
            dve.tensor_tensor(wab[:, 1, :], w_stage[:, 0:2 * H], wab[:, 0, :].bitcast(F32), ALU.subtract
                              ).then_inc(s_split, 1)
            dve.tensor_tensor(w2[:, 1, :, :].rearrange("p k h -> p (k h)"), w_stage[:, 2 * H:4 * H],
                              w2[:, 0, :, :].rearrange("p k h -> p (k h)").bitcast(F32), ALU.subtract
                              ).then_inc(s_split, 1)
            dve.tensor_tensor(rows_lo[0:2, :, :], rows_in[0:2, :, :], rows_hi[0:2, :, :], ALU.subtract
                              ).then_inc(s_lo, 1)
            dve.wait_ge(s_lo, 1)

            dve.tensor_scalar(rows_hi[0:2, :, :], rows_hi[0:2, :, :], ident[0:2, 0:1], None, ALU.mult
                              ).then_inc(s_lo, 1)
            dve.wait_ge(s_lo, 2)
            for a, rows in enumerate((b1_rows, b2_rows)):
                for j in range(2):
                    dve.scalar_tensor_tensor(rows[:, j * H:(j + 1) * H], rows_lo[0:2, a, :], ident[0:2, 1:2],
                                             rows_hi[0:2, a, :], ALU.mult, ALU.add).then_inc(s_split, 1)
            dve.wait_ge(s_edges, 16 * len(loads))
            dve.tensor_copy(edges_f[0:BG, :], edges_in[0:BG, :]).then_inc(s_ef, 1)
            dve.tensor_copy(edges16[0:BG, :], edges_in[0:BG, 0:GR * EB]).then_inc(s_d16, 1)
            dve.wait_ge(s_ef, 1)
            dst_f = edges_f[0:BG, 0:GR * EB].rearrange("b (g e) -> b g e", g=GR)
            for n, op in enumerate((ALU.min, ALU.max)):
                dve.tensor_reduce(minmax[0:BG, n:2 * GR:2], dst_f, AX.X, op).then_inc(s_mm, 1)
            dve.wait_ge(s_mm, 2)
            dve.tensor_copy(minmax_i[0:BG, :], minmax[0:BG, :]).then_inc(s_wi, 1)
            dve.wait_ge(s_wi, 1)
            dve.tensor_single_scalar(win_i[0:BG, :], minmax_i[0:BG, :], 7, ALU.arith_shift_right
                                     ).then_inc(s_win, 1)
            for n, col in enumerate((dst_col, src_idx)):
                for g in range(GR):
                    dve.wait_ge(s_et, n * GR + g + 1)
                    dve.tensor_copy(col[:, g * BG * TB:(g + 1) * BG * TB].rearrange("p (b t) -> p t b", t=TB),
                                    bank[n * GR + g][:, 0:TB * BG].rearrange("p (t b) -> p t b", t=TB)
                                    ).then_inc(s_ec, 1)

            def tables(g, k, half):
                n = size(g)
                if n:
                    dve.wait_ge(s_xh, g + 1)
                    dve.tensor_tensor(xl[:, k, 0:n * P], bank[k][:, 0:n * P], xh[:, k, 0:n * P].bitcast(F32),
                                      ALU.subtract).then_inc(s_xl, 1)
                n = size(g, 1)
                for q in range((n + 1) // 2):
                    m = min(n - 2 * q, 2)
                    dve.wait_ge(s_bh, g * 2 - 2 + (q + 1))
                    both = b_tab[:, bass.ds(g * GW - GW + 2 * q, m), :, :]
                    dve.tensor_tensor(both[:, :, 1, :], bank[4 + q][:, 0:m * H].rearrange("p (w h) -> p w h", h=H),
                                      both[:, :, 0, :], ALU.subtract).then_inc(s_bl, 1)
            groups(dve, tables, 1)
            dve.wait_ge(s_bl, NPAIR)
            for k in range(2):
                dve.wait_ge(s_as[k], 16 * ((NG + 1 - k) // 2))
            dve.wait_ge(s_row, 16)
            more_t = dve.alloc_register("further_pairs_expand")
            more = dve.alloc_register("further_pairs_sum")
            dve.reg_mov(more_t, 1)
            dve.reg_mov(more, 0)

            def make_onehot_t(slot, k, w):
                at = k % 2 * EB
                dve.tensor_scalar(onehot_t[:, slot, :], dst_all[:, k % U // 2, at:at + EB],
                                  node_id[:, bass.ds(w, 1)], None, ALU.is_equal).then_inc(s_ot[slot], 1)

            def make_second_onehot_t(k, lo, hi):
                with dve.If(lo < hi):
                    dve.reg_add(more_t, more_t, 1)
                    make_onehot_t(1, k, after(lo))

            def make_onehot(slot, i, k, w):
                for t in range(TB):
                    ins = dve.tensor_scalar(onehot[:, slot, t, :], iota16[:, :], first_node[:, bass.ds(w, 1)],
                                            dst_col[:, bass.ds(i * (U * TB) + (k * TB + t), 1)],
                                            ALU.add, ALU.is_equal)
                ins.then_inc(s_oh[slot], 1)

            def make_further_onehot(i, k, w):
                dve.reg_add(more, more, 1)
                make_onehot(1, i, k, w)

            def add_sums(slot, w):
                sums = agg[:, bass.ds(w * HC, HC)]
                dve.tensor_tensor(sums, bank[4 + slot][:, 0:HC], sums, ALU.add)

            def body(i):
                win = load_windows(dve, i)
                if isinstance(i, int) and i == 0:
                    dve.wait_ge(s_da[0], 16)
                    make_onehot_t(0, 0, win[0][0])
                    make_second_onehot_t(0, *win[0])
                    dve.memset(agg[:, :], 0.0).then_inc(s_zero, 1)
                    dve.wait_ge(s_zero, 1)
                for k in steps(i):
                    if there(i, k):
                        lo, hi = win[k]
                        with dve.If(lo + 1 < hi):
                            with dve.Fori(lo + 2, hi + 1) as w:
                                dve.wait_ge(s_ex[1], more_t)
                                dve.reg_add(more_t, more_t, 1)
                                make_onehot_t(1, k, w)
                        if there(i, k + 1):
                            if (k + 1) % 2 == 0:
                                dve.wait_ge(s_da[(k + 1) % U // 2], i * 16 + 16 * ((k + 1) // U + 1))
                            dve.wait_ge(s_ex[0], i * U + (k + 1))
                            make_onehot_t(0, k + 1, win[k + 1][0])
                        dve.wait_ge(s_h1h, i * U + (k + 1))
                        dve.scalar_tensor_tensor(h1[:, k % 2, 1, :], bank[k % 2][:, :], 0.0,
                                                 h1[:, k % 2, 0, :].bitcast(F32), ALU.max, ALU.subtract
                                                 ).then_inc(s_h1l, 1)
                        if there(i, k + 1):
                            make_second_onehot_t(k + 1, *win[k + 1])
                    if there(i, k - 1):
                        dve.wait_ge(s_h2h, i * U + k)
                        dve.scalar_tensor_tensor(h2_lo[:, (k - 1) % 2, :, :],
                                                 bank[2 + (k - 1) % 2][:, :].rearrange("p (t h) -> p t h", t=TB),
                                                 0.0, h2_hi[:, (k - 1) % 2, :, 0:H].bitcast(F32),
                                                 ALU.max, ALU.subtract).then_inc(s_h2l, 1)
                    if there(i, k - 2):
                        lo, hi = win[k - 2]
                        dve.wait_ge(s_sg[0], i * U + (k - 1))
                        add_sums(0, lo)
                        with dve.If(lo < hi):
                            dve.wait_ge(s_sg[1], more)
                            add_sums(1, after(lo))
                        with dve.If(lo + 1 < hi):
                            with dve.Fori(lo + 2, hi + 1) as w:
                                make_further_onehot(i, k - 2, w)
                                dve.wait_ge(s_sg[1], more)
                                add_sums(1, w)
                    if there(i, k - 1):
                        lo, hi = win[k - 1]
                        make_onehot(0, i, k - 1, lo)
                        with dve.If(lo < hi):
                            make_further_onehot(i, k - 1, after(lo))
            bodies(dve, body)
            dve.engine_nop().then_inc(s_end, 1)

            agg3 = agg[:, :].rearrange("p (w c) -> p w c", c=HC)

            def reciprocal_counts(g, k, n):
                dve.tensor_scalar(f_cnt[:, k, 0:n], agg3[:, bass.ds(g * GW, n), H:H + 1]
                                  .rearrange("p w o -> p (w o)"), 1.0, None, ALU.max).then_inc(s_f1, 1)
                dve.wait_ge(s_f1, g + 1)
                dve.reciprocal(f_rec[:, k, 0:n], f_cnt[:, k, 0:n]).then_inc(s_f2, 1)

            def means(g, k, n):
                for j in range(n):
                    ins = dve.tensor_scalar(f_mean[:, k, j, :], agg[:, bass.ds((g * GW + j) * HC, HC)],
                                            f_rec[:, k, j:j + 1], None, ALU.mult)
                ins.then_inc(s_fm, 1)

            reciprocal_counts(0, 0, size(0))
            dve.wait_ge(s_f2, 1)
            means(0, 0, size(0))
            dve.wait_ge(s_fbh, 1)
            dve.tensor_tensor(f_bias_lo[0:2, :], f_bias_in[0:2, :], f_bias_hi[0:2, :], ALU.subtract
                              ).then_inc(s_fbl, 1)
            dve.wait_ge(s_fbl, 1)
            dve.tensor_scalar(f_bias_hi[0:2, :], f_bias_hi[0:2, :], ident[0:2, 0:1], None, ALU.mult
                              ).then_inc(s_fbl, 1)
            dve.wait_ge(s_fbl, 2)
            for to, a in [(b3_rows, 0)] + [(bn2_rows[:, j * D:(j + 1) * D], D) for j in range(GW)]:
                dve.scalar_tensor_tensor(to, f_bias_lo[0:2, a:a + D], ident[0:2, 1:2], f_bias_hi[0:2, a:a + D],
                                         ALU.mult, ALU.add).then_inc(s_fbr, 1)

            def final(g, k, half):
                ahead = size(g, -1)
                if ahead:
                    reciprocal_counts(g + 1, 1 - k, ahead)
                n = size(g, 4)
                if n:
                    dve.wait_ge(s_fu, g - 3)
                    if used(g, 4):
                        dve.wait_ge(s_fo, g - 5)
                    y = f_y[:, k, 0:n * D]
                    dve.scalar_tensor_tensor(y.rearrange("p (w d) -> p w d", d=D),
                                             f_x[:, bass.ds(g * GW - 4 * GW, n), :], 2.0,
                                             bank[7][:, 0:n * D].rearrange("p (w d) -> p w d", d=D),
                                             ALU.mult, ALU.add).then_inc(s_fy, 1)
                    dve.wait_ge(s_fy, g - 3)
                    for j in range(n):
                        dve.bn_stats(f_bn[:, k, j, :], y[:, j * D:(j + 1) * D]).then_inc(s_fn, 1)
                    if n < GW or isinstance(g, int):
                        dve.wait_ge(s_fn, GW * (g - 4) + n)
                    else:
                        dve.wait_ge(s_fn, g * GW - 3 * GW)
                if ahead:
                    dve.wait_ge(s_f2, g + 2)
                    if used(g, -1):
                        dve.wait_ge(s_fmt, g)
                    means(g + 1, 1 - k, ahead)
                if n:
                    for j in range(n):
                        dve.bn_aggr(f_mv[:, k, j, :], f_bn[:, k, j, :]).then_inc(s_fv, 1)
                    if n < GW or isinstance(g, int):
                        dve.wait_ge(s_fv, GW * (g - 4) + n)
                    else:
                        dve.wait_ge(s_fv, g * GW - 3 * GW)
                    dve.tensor_scalar(f_ve[:, k, 0:n], f_mv[:, k, 0:n, 1:2].rearrange("p w o -> p (w o)"),
                                      EPS, None, ALU.add).then_inc(s_fe, 1)
                n = size(g)
                if n:
                    dve.wait_ge(s_fmt, g + 1)
                    if used(g):
                        dve.wait_ge(s_fg, g - 1)
                    dve.tensor_copy(f_feat[:, k, 1, 0:n * P], bank[1][:, 0:n * P])
                    dve.tensor_copy(f_row[k][:, 0:n * P], bank[3][0:2, 0:n * P]).then_inc(s_fr, 1)
                n = size(g, 5)
                if n:
                    j = 1 - k
                    dve.wait_ge(s_fs, g - 4)
                    dve.reciprocal(f_rs[:, j, 0:n], f_sd[:, j, 0:n]).then_inc(s_fq, 1)
                    dve.wait_ge(s_fq, g - 4)
                    if used(g, 5):
                        dve.wait_ge(s_fst[j], ((g - 5) // 2 if isinstance(g, int) else half - 3 + k) * 16)
                    for w in range(n):
                        ins = dve.tensor_scalar(f_out[:, j, w, :], f_y[:, j, w * D:(w + 1) * D],
                                                f_mv[:, j, w, 0:1], f_rs[:, j, w:w + 1], ALU.subtract, ALU.mult)
                    ins.then_inc(s_fo, 1)
            dve.wait_ge(s_fx, 16 * 9)
            groups(dve, final, 5, 1)

        @block.tensor
        def _(pe):
            pe.wait_ge(s_const, 9)
            pe.wait_ge(s_ef, 1)
            for n in range(2):
                for g in range(GR):
                    for t in range(TB):
                        at = (n * GR + g) * EB + t * P
                        ins = pe.transpose(bank[n * GR + g][:, t * BG:(t + 1) * BG], edges_f[0:BG, at:at + P],
                                           ident[0:BG, 0:BG])
                    ins.then_inc(s_et, 1)
            pe.wait_ge(s_ec, 2 * GR)
            pe.wait_ge(s_split, 6)

            def tables(g, k, half):
                n = size(g)
                if n:
                    extra = 1 if n < GW and n > 1 else 0
                    pe.wait_ge(s_xs[k], 16 * (half + 1 + extra))
                    if used(g):
                        pe.wait_ge(s_xl, g - 1)
                    for j in range(n):
                        ins = pe.transpose(bank[k][:, j * P:(j + 1) * P], x_slot[:, k, j, :], ident[:, :])
                    ins.then_inc(s_xt, 1)
                n = size(g, 1)
                if n:
                    pe.wait_ge(s_xl, g)
                for q in range((n + 1) // 2):
                    m = min(n - 2 * q, 2)
                    if used(g, 0):
                        pe.wait_ge(s_ac, g * 2 - 4 + (q + 1))
                        pe.wait_ge(s_bl, g * 2 - 4 + (q + 1))
                    pe.matmul(bank[4 + q][:, 0:m * H], ones2[:, :], b1_rows[:, 0:m * H], start=True, stop=False,
                              skip_group_check=True)
                    for w in range(m):
                        v = slice((2 * q + w) * P, (2 * q + w + 1) * P)
                        for c in range(2):
                            for n_, (xp, a) in enumerate(((xh, 0), (xh, 1), (xl, 0))):
                                ins = pe.matmul(bank[2 + 2 * c + q][:, w * H:(w + 1) * H], xp[:, 1 - k, v],
                                                wab[:, a, c * H:(c + 1) * H],
                                                start=(c == 0 and w == 0 and n_ == 0), stop=(n_ == 2),
                                                skip_group_check=True)
                    ins.then_inc(s_ab, 1)
            groups(pe, tables, 1)
            pe.wait_ge(s_row, 16)
            pe.wait_ge(s_ac, NPAIR)
            pe.wait_ge(s_bl, NPAIR)
            more_t = pe.alloc_register("further_pairs_expand_pe")
            more = pe.alloc_register("further_pairs_sum_pe")
            pe.reg_mov(more_t, 0)
            pe.reg_mov(more, 0)
            pe.nop().then_inc(s_ex[1], 1)

            def expand(slot, k):
                for h in range(KH):
                    for a in range(2):
                        ins = pe.matmul(bank[k % 2][:, h * EB:(h + 1) * EB], b_win[:, slot, a, h * P:(h + 1) * P],
                                        onehot_t[:, slot, :], start=False, stop=True, skip_group_check=True)
                ins.then_inc(s_ex[slot], 1)

            def expand_further(k):
                pe.reg_add(more_t, more_t, 1)
                pe.wait_ge(s_ot[1], more_t)
                pe.wait_ge(s_bw[1], more_t)
                expand(1, k)

            def sum_segments(slot, k):
                to = bank[4 + slot]
                for t in range(TB):
                    pe.matmul(to[:, 0:HC], onehot[:, slot, t, :], h2_hi[:, k % 2, t, :], start=(t == 0),
                              stop=False, skip_group_check=True)
                    ins = pe.matmul(to[:, 0:H], onehot[:, slot, t, :], h2_lo[:, k % 2, t, :], start=False,
                                    stop=(t == TB - 1), skip_group_check=True)
                ins.then_inc(s_sg[slot], 1)

            def sum_further(k):
                pe.reg_add(more, more, 1)
                pe.wait_ge(s_oh[1], more)
                sum_segments(1, k)

            def body(i):
                win = load_windows(pe, i)
                for k in steps(i):
                    if there(i, k):
                        for t in range(TB):
                            pe.wait_ge(s_g[k * TB + t], i * 16 + 16)
                            for h in range(KH):
                                ins = pe.matmul(bank[k % 2][:, h * EB + t * P:h * EB + (t + 1) * P],
                                                a_edge[:, k * TB + t, h * P:(h + 1) * P], ident[:, :],
                                                start=(t == 0 and h == 0), stop=False, is_transpose=True,
                                                skip_group_check=True)
                        ins.then_inc(s_ta, 1)
                        pe.wait_ge(s_ot[0], i * U + (k + 1))
                        pe.wait_ge(s_bw[0], i * U + (k + 1))
                        expand(0, k)
                        further(pe, *win[k], lambda w: expand_further(k))
                    if there(i, k - 1):
                        j = (k - 1) % 2
                        pe.wait_ge(s_h1l, i * U + k)
                        pe.matmul(bank[2 + j][:, :], ones2[:, :], b2_rows[:, :], start=True, stop=False,
                                  skip_group_check=True)
                        for t in range(TB):
                            to = bank[2 + j][:, t * H:(t + 1) * H]
                            for a, b in ((0, 0), (0, 1), (1, 0)):
                                for h in range(KH):
                                    ins = pe.matmul(to, h1[:, j, a, h * EB + t * P:h * EB + (t + 1) * P],
                                                    w2[:, b, h, :], start=False, stop=(a == 1 and h == KH - 1),
                                                    skip_group_check=True)
                        ins.then_inc(s_w2, 1)
                    if there(i, k - 2):
                        pe.wait_ge(s_h2l, i * U + (k - 1))
                        pe.wait_ge(s_oh[0], i * U + (k - 1))
                        sum_segments(0, k - 2)
                        further(pe, *win[k - 2], lambda w: sum_further(k - 2))
            bodies(pe, body)
            pe.wait_ge(s_fx, 16 * 9)
            pe.wait_ge(s_fbr, 1 + GW)

            def final(g, k, half):
                n = size(g)
                if n:
                    pe.wait_ge(s_fm, g + 1)
                    pe.wait_ge(s_fxs, g + 1)
                    if not isinstance(g, int) or g >= 1:
                        pe.wait_ge(s_fcx, g)
                        pe.wait_ge(s_fr, g)
                    for w in range(n):
                        v = slice(w * P, (w + 1) * P)
                        for h in range(KH):
                            pe.transpose(bank[h][:, v], f_mean[:, k, w, h * P:(h + 1) * P], ident[:, :])
                        pe.transpose(bank[2][:, v], f_xs[:, k, w, :], ident[:, :])
                        ins = pe.transpose(bank[3][0:2, v], f_mean[:, k, w, H:HC], ident[:, :])
                    ins.then_inc(s_fmt, 1)
                j = 1 - k
                n = size(g, 1) * P
                if n:
                    pe.wait_ge(s_fc, g)
                    pe.wait_ge(s_fr, g)
                    if used(g):
                        pe.wait_ge(s_fa, g - 1)
                    for h in range(KH):
                        pe.matmul(bank[4][:, 0:n], w3[:, h, :], f_feat[:, j, h, 0:n], start=(h == 0), stop=False)
                    pe.matmul(bank[4][:, 0:n], b3_rows, f_row[j][:, 0:n], start=False, stop=True
                              ).then_inc(s_fg, 1)
                n = size(g, 2) * P
                if n:
                    pe.wait_ge(s_fa, g - 1)
                    pe.wait_ge(s_fcx, g - 1)
                    if used(g, 1):
                        pe.wait_ge(s_fhr, g * 2 - 4)
                    for h in range(KH):
                        to = bank[5 + h][:, 0:n]
                        pe.matmul(to, wn1[:, 0, h * P:(h + 1) * P], f_feat[:, k, 2, 0:n], start=True, stop=False)
                        ins = pe.matmul(to, wn1[:, 1, h * P:(h + 1) * P], f_msg[:, k, 0:n], start=False, stop=True)
                    ins.then_inc(s_fh, 1)
                n = size(g, 3)
                if n:
                    pe.wait_ge(s_fhr, g * 2 - 4)
                    if used(g, 2):
                        pe.wait_ge(s_fy, g - 3)
                    pe.matmul(bank[7][:, 0:n * D], ones2[:, :], bn2_rows[:, 0:n * D], start=True, stop=False,
                              skip_group_check=True)
                    for w in range(n):
                        for h in range(KH):
                            ins = pe.matmul(bank[7][:, w * D:(w + 1) * D], f_hid[:, j, h, w * P:(w + 1) * P],
                                            wn2[:, h, :], start=False, stop=(h == KH - 1), skip_group_check=True)
                    ins.then_inc(s_fu, 1)
            groups(pe, final, 3)


_INS = ["x", "src", "dst"] + ["L0_gnn_" + n for n in
                              ("Wm1", "bm1", "Wm2", "bm2", "Wm3", "bm3", "Wn1", "bn1", "Wn2", "bn2")]


def kernel(**inputs):
    import numpy as np
    import concourse.bacc as bacc
    from concourse.bass_utils import run_bass_kernel_spmd

    nc = bacc.Bacc("TRN2", target_bir_lowering=False, num_devices=1)
    arrays, args = {}, []
    for name in _INS:
        a = np.ascontiguousarray(inputs[name])
        arrays[f"in_{name}"] = a
        args.append(nc.dram_tensor(f"in_{name}", a.shape, mybir.dt.from_np(a.dtype), kind="ExternalInput").ap())
    shape = inputs["x"].shape
    args.append(nc.dram_tensor("out_0", shape, F32, kind="ExternalOutput").ap())
    gnn_layer(nc, *args)
    r = run_bass_kernel_spmd(nc, [arrays], core_ids=[0])
    return r.results[0]["out_0"]
```

```python
from contextlib import ExitStack

import numpy as np

import concourse.bass as bass
from concourse import mybir

F32 = mybir.dt.float32
F32R = mybir.dt.float32r
I32 = mybir.dt.int32
I16 = mybir.dt.int16
ALU = mybir.AluOpType
ACT = mybir.ActivationFunctionType
AX = mybir.AxisListType

P = 128
TB = 2
EB = TB * P
U = 8
R = 4
MORE = 2
EPS = 1e-5


def gnn_layer(nc, x, src, dst, Wm1, bm1, Wm2, bm2, Wm3, bm3, Wn1, bn1, Wn2, bn2, out):
    N, D = x.shape
    (E,) = src.shape
    H = Wm1.shape[1]
    KH = H // P
    NW = -(-N // P)
    NLAST = N - (NW - 1) * P
    NB = -(-E // EB)
    NB = -(-NB // U) * U
    GR = 4
    BG = NB // GR
    NI = NB // U
    PAD_DST = NW * P - 1
    GW = 4
    NG = -(-NW // GW)
    HC = H + 2
    assert D == P and H == 2 * P and BG <= P and NI >= 3 and NW >= 4 and NW * P > N

    a_table = nc.dram_tensor("a_table", [NW * P, H], F32, kind="Internal").ap()
    dst16_dram = nc.dram_tensor("dst16_dram", [NB, EB], I16, kind="Internal").ap()
    win_dram = nc.dram_tensor("win_dram", [NB, 2], I32, kind="Internal").ap()

    with ExitStack() as ctx:
        def sb(name, shape, dt):
            return ctx.enter_context(nc.sbuf_tensor(name, shape, dt))

        def sem(name):
            return ctx.enter_context(nc.semaphore(name))

        b_tab = sb("b_tab", [P, NW, 2, H], F32)
        agg = sb("agg", [P, NW * HC], F32)
        iota16 = sb("iota16", [P, TB, P], I16)
        first_node = sb("first_node", [P, NW], F32)
        node_id = sb("node_id", [P, NW], F32)
        src_idx = sb("src_idx", [P, NB * TB], I32)
        dst_col = sb("dst_col", [P, NB * TB], F32)
        win_row = sb("win_row", [1, 2 * (NB + 8)], I32)
        w2 = sb("w2", [P, 2, KH, H], F32R)
        b2_bc = sb("b2_bc", [P, TB, H], F32)
        b3_rows = sb("b3_rows", [2, D], F32R)
        bn2_rows = sb("bn2_rows", [2, D], F32R)
        w3 = sb("w3", [P, KH, D], F32)
        wn1 = sb("wn1", [P, 2, H], F32)
        wn2 = sb("wn2", [P, KH, D], F32)
        bn1_col = sb("bn1_col", [P, KH], F32)
        ones2 = sb("ones2", [2, P], F32R)
        ident = sb("ident", [P, P], F32)
        a_edge = sb("a_edge", [P, R * TB, H], F32)
        idx_now = sb("idx_now", [P, R * TB], I32)
        zero_idx = sb("zero_idx", [P, TB], I32)
        dst_all = sb("dst_all", [P, 2, 2 * EB], I16)
        onehot_t = sb("onehot_t", [P, 3, EB], F32R)
        b_win = sb("b_win", [P, 3, 2, H], F32R)
        onehot = sb("onehot", [P, 3, TB, P], F32R)
        h1 = sb("h1", [P, 2, 2, KH * EB], F32R)
        h2_hi = sb("h2_hi", [P, 2, TB, HC], F32R)
        h2_lo = sb("h2_lo", [P, 2, TB, H], F32R)

        bank = [ctx.enter_context(nc.psum_tensor(f"bank{i}", [P, 512], F32)) for i in range(8)]

        wab = h1[:, 0, :, :]
        xl = h1[:, 1, :, :]
        xh = h2_lo[:, :, :, :].rearrange("p s t h -> p s (t h)")
        b1_rows = b_win[0:2, 2, :, :].rearrange("p a h -> p (a h)")
        edges_in = a_edge[:, :, :].rearrange("p a h -> p (a h)").bitcast(I32)

        class Carve:
            def __init__(self, region, limit):
                self.region, self.at, self.limit = region, 0, limit

            def __call__(self, *shape):
                cols = int(np.prod(shape))
                v = self.region[:, self.at:self.at + cols]
                self.at += cols
                assert self.at <= self.limit
                if len(shape) == 2:
                    return v.rearrange("p (a b) -> p a b", a=shape[0])
                if len(shape) == 3:
                    return v.rearrange("p (a b c) -> p a b c", a=shape[0], b=shape[1])
                return v

        carve = Carve(agg, NW * HC)
        edges_f = carve(2 * GR * EB)
        edges16 = carve(GR * EB // 2).bitcast(I16)
        rows_in = carve(H + 2 * D)
        rows_hi = carve(H + 2 * D)
        rows_lo = carve(H + 2 * D)
        minmax = carve(2 * GR)
        minmax_i = carve(2 * GR).bitcast(I32)
        win_i = carve(2 * GR).bitcast(I32)
        zero_by_dve = carve.at
        w_stage = carve(4 * H)
        x_slot = carve(2, GW, D)
        a_out = carve(2, GW, H)
        carve = Carve(b_tab[:, :, :, :].rearrange("p w a h -> p (w a h)"), NW * 2 * H)
        f_x = carve(NW, D)
        f_xs = carve(2, GW, D)
        f_cnt, f_rec = carve(2, GW), carve(2, GW)
        f_mean = carve(2, GW, HC)
        f_feat = carve(2, 3, GW * P)
        f_msg = carve(2, GW * P)
        f_hid = carve(2, KH, GW * P)
        f_y, f_out = carve(2, GW * D), carve(2, GW, D)
        f_bn, f_mv = carve(2, GW, 6), carve(2, GW, 2)
        f_ve, f_sd, f_rs = carve(2, GW), carve(2, GW), carve(2, GW)
        f_row = [h1[0:2, k, 0, :] for k in range(2)]

        s_w = sem("s_weights_loaded")
        s_b2 = sem("s_b2_loaded")
        s_w2in = sem("s_w2_loaded")
        s_w2s = sem("s_w2_split")
        s_edges = sem("s_edges_loaded")
        s_pad = sem("s_padding_set")
        s_zeros = sem("s_ident_zeroed")
        s_const = sem("s_constants")
        s_hi = sem("s_weights_hi")
        s_lo = sem("s_bias_parts")
        s_split = sem("s_weights_split")
        s_ef = sem("s_edges_as_float")
        s_mm = sem("s_min_max")
        s_wi = sem("s_min_max_int")
        s_win = sem("s_windows_found")
        s_d16 = sem("s_dst16_made")
        s_scr = sem("s_scratch_stored")
        s_row = sem("s_win_row_loaded")
        s_et = sem("s_edges_transposed")
        s_ec = sem("s_edge_columns")
        s_xs = [sem(f"s_x_in_slot{k}") for k in range(2)]
        s_xz = sem("s_last_x_zeroed")
        s_xt = sem("s_x_transposed")
        s_xh = sem("s_x_hi")
        s_xl = sem("s_x_lo")
        s_ab = sem("s_ab_product")
        s_ac = sem("s_a_copied")
        s_as = [sem(f"s_a_stored{k}") for k in range(2)]
        s_bh = sem("s_b_hi")
        s_bl = sem("s_b_lo")
        s_zero = sem("s_agg_zeroed")
        s_idx = sem("s_idx_copied")
        s_g = [sem(f"s_gathered{t}") for t in range(R * TB)]
        s_da = [sem(f"s_dst_all{c}") for c in range(2)]
        s_ta = sem("s_a_transposed")
        s_ot = [sem(f"s_onehot_t_made{k}") for k in range(2)]
        s_bw = [sem(f"s_b_win_copied{k}") for k in range(2)]
        s_ex = [sem(f"s_expanded{k}") for k in range(2)]
        s_h1h = sem("s_h1_hi")
        s_h1l = sem("s_h1_lo")
        s_w2 = sem("s_h2_product")
        s_bits = sem("s_banks_written")
        s_seed = sem("s_b2_in_bank")
        s_h2h = sem("s_h2_hi")
        s_h2l = sem("s_h2_lo")
        s_oh = [sem(f"s_onehot_made{k}") for k in range(2)]
        s_sg = [sem(f"s_segments_summed{k}") for k in range(2)]
        s_add = sem("s_sums_added")
        s_fz = sem("s_final_x_zeroed")
        s_fw = sem("s_final_weights_loaded")
        s_fx = [sem(f"s_final_x_loaded{q}") for q in range(2)]
        s_f1 = sem("s_count_clamped")
        s_f2 = sem("s_count_inverted")
        s_fm = sem("s_mean")
        s_fxs = sem("s_final_x_in_slot")
        s_fmt = sem("s_mean_transposed")
        s_fc = sem("s_features_copied")
        s_fcx = sem("s_final_x_copied")
        s_fr = sem("s_mask_row")
        s_fg = sem("s_message_product")
        s_fa = sem("s_message_copied")
        s_fh = sem("s_hidden_product")
        s_fhr = sem("s_hidden_relu")
        s_fu = sem("s_update_product")
        s_fy = sem("s_residual_added")
        s_fn = sem("s_bn_stats")
        s_fv = sem("s_mean_variance")
        s_fe = sem("s_variance_eps")
        s_fs = sem("s_std")
        s_fq = sem("s_std_inverted")
        s_fo = sem("s_normalised")
        s_fst = [sem(f"s_out_stored{k}") for k in range(2)]

        def groups(e, step, lag, ahead=0, peel=0):
            first = lag + 2 + peel
            count = (NG - 1 - ahead - first) // 2
            for g in range(first):
                step(g, g % 2, g // 2)
            with e.Fori(0, count) as i:
                for k in range(2):
                    step(i * 2 + (first + k), (first + k) % 2, i + (first + k) // 2)
            for g in range(first + 2 * count, NG + lag):
                step(g, g % 2, g // 2)

        def size(g, back=0):
            if isinstance(g, int) and not 0 <= g - back < NG:
                return 0
            return NW - (NG - 1) * GW if isinstance(g, int) and g - back == NG - 1 else GW

        def used(g, back=0):
            return not isinstance(g, int) or g - back >= 2

        def load_x(e, g, n, to, done):
            whole = n if not (isinstance(g, int) and g == NG - 1) else n - 1
            if whole:
                e.dma_start(to[:, 0:whole, :], x[bass.ds(g * (GW * P), whole * P), :]
                            .rearrange("(w p) d -> p w d", p=P)).then_inc(done, 16)
            if whole < n:
                e.dma_start(to[0:NLAST, whole, :], x[N - NLAST:N, :]).then_inc(done, 16)

        def bodies(e, body):
            body(0)
            with e.Fori(1, NI - 1) as i:
                body(i)
            body(NI - 1)

        def there(i, k):
            return not isinstance(i, int) or 0 <= U * i + k < NB

        def uses(i, k):
            return i * (U // R) + k // R

        def load_windows(e, i):
            vals = nc.values_load_multi_w_load_instructions(
                win_row[0:1, bass.ds(i * (2 * U), 2 * (U + 4))], engines=[e.engine], min_val=0, max_val=NW - 1,
                skip_runtime_bounds_check_because="dst is a node's number")[1]
            return {k: (vals[2 * k + 4], vals[2 * k + 5]) for k in range(-2, U + 2)}

        def further(e, lo, hi, step):
            with e.If(lo < hi):
                with e.Fori(lo + 1, hi + 1) as w:
                    step(w)

        def after(lo):
            return nc.s_assert_within(lo + 1, 1, NW - 1, skip_runtime_bounds_check_because="lo < hi")

        def steps(i):
            return range(U + 2) if isinstance(i, int) and i == NI - 1 else range(U)

        full = E // EB
        assert (GR - 1) * BG <= full
        loads = []
        for n in range(2):
            for g in range(GR):
                rows = min(full - g * BG, BG)
                if rows:
                    loads.append((n, g, 0, rows, EB))
            if E % EB:
                loads.append((n, GR - 1, rows, 1, E % EB))

        NPAIR = 2 * (NG - 1) + (size(NG - 1) + 1) // 2

        block = ctx.enter_context(nc.Block())

        @block.sync
        def _(sp):
            for g in range(2):
                load_x(sp, g, GW, x_slot[:, g, :, :], s_xs[g])
            sp.wait_ge(s_pad, 2)
            for n, g, row, rows, edges in loads:
                at, e0 = (n * GR + g) * EB, (g * BG + row) * EB
                sp.dma_start(edges_in[row:row + rows, at:at + edges],
                             (dst, src)[n][e0:e0 + rows * edges].rearrange("(b e) -> b e", e=edges)
                             ).then_inc(s_edges, 16)
            def edges_out():
                sp.wait_ge(s_win, 1)
                sp.wait_ge(s_d16, 1)
                for g in range(GR):
                    sp.dma_start(win_dram[g * BG:(g + 1) * BG, :], win_i[0:BG, 2 * g:2 * g + 2]).then_inc(s_scr, 16)
                    sp.dma_start(dst16_dram[g * BG:(g + 1) * BG, :],
                                 edges16[0:BG, g * EB:(g + 1) * EB]).then_inc(s_scr, 16)

            def tables(g, k, half):
                if isinstance(g, int) and g == NG - 1:
                    edges_out()
                if size(g) and used(g):
                    sp.wait_ge(s_xt, g - 1)
                    if size(g) < GW:
                        sp.wait_ge(s_xz, 1)
                    load_x(sp, g, size(g), x_slot[:, k, :, :], s_xs[k])
                n = size(g, 2)
                if n:
                    sp.wait_ge(s_ac, g * 2 - 2 if n > 2 else g * 2 - 3)
                    sp.dma_start(a_table[bass.ds((g - 2) * (GW * P), n * P), :]
                                 .rearrange("(w p) h -> p w h", p=P), a_out[:, k, 0:n, :]).then_inc(s_as[k], 16)
            groups(sp, tables, 2)
            sp.wait_ge(s_scr, 32 * GR)
            sp.dma_start(win_row[0:1, 4:4 + 2 * NB], win_dram.rearrange("(o b) c -> o (b c)", o=1)
                         ).then_inc(s_row, 16)
            sp.dma_start(w3[:, :, :], Wm3.rearrange("(k p) d -> p k d", p=P)).then_inc(s_fw, 16)
            sp.dma_start(wn1[:, :, :], Wn1.rearrange("(k p) d -> p k d", p=P)).then_inc(s_fw, 16)
            sp.dma_start(wn2[:, :, :], Wn2.rearrange("(k p) d -> p k d", p=P)).then_inc(s_fw, 16)
            for k in range(KH):
                sp.dma_start(bn1_col[:, k:k + 1], bn1[k * P:(k + 1) * P].rearrange("(p o) -> p o", o=1)
                             ).then_inc(s_fw, 16)

            def body(i):
                for c in range(U // 2):
                    if there(i, 2 * c - 4):
                        sp.wait_ge(s_h1l, i * U + (2 * c - 2))
                    sp.dma_start(dst_all[:, c % 2, :].rearrange("p (b e) -> p b e", b=2),
                                 dst16_dram[bass.ds(i * U + 2 * c, 2), :].partition_broadcast(P)
                                 ).then_inc(s_da[c % 2], 16)
            bodies(sp, body)

            sp.wait_ge(s_h1h, NB)
            for q, (a, b) in enumerate(((0, 2 * GW), (2 * GW, NW - 1))):
                sp.dma_start(f_x[:, a:b, :], x[a * P:b * P, :].rearrange("(w p) d -> p w d", p=P)
                             ).then_inc(s_fx[q], 16)
            sp.wait_ge(s_fz, 1)
            sp.dma_start(f_x[0:NLAST, NW - 1, :], x[(NW - 1) * P:N, :]).then_inc(s_fx[1], 16)

            def store_out(g, k, half):
                n = size(g)
                sp.wait_ge(s_fo, g + 1)
                whole = n - 1 if isinstance(g, int) and g == NG - 1 else n
                if whole:
                    sp.dma_start(out[bass.ds(g * (GW * P), whole * P), :].rearrange("(w p) d -> p w d", p=P),
                                 f_out[:, k, 0:whole, :]).then_inc(s_fst[k], 16)
                if whole < n:
                    sp.dma_start(out[N - NLAST:N, :], f_out[0:NLAST, k, whole, :]).then_inc(s_fst[k], 16)
            groups(sp, store_out, 0)
            last = (NG - 1) % 2
            for k in range(2):
                sp.wait_ge(s_fst[k], 16 * ((NG + 1 - k) // 2 + (k == last and size(NG - 1) > 1)))

        @block.gpsimd
        def _(pool):
            pool.memset(edges_in[:, (GR - 1) * EB:GR * EB], PAD_DST).then_inc(s_pad, 1)
            pool.memset(edges_in[:, (2 * GR - 1) * EB:2 * GR * EB], 0).then_inc(s_pad, 1)
            pool.memset(ident[:, :], 0.0).then_inc(s_zeros, 1)
            pool.wait_ge(s_zeros, 1)
            pool.affine_select(out=ident[:, :], in_=ident[:, :], compare_op=ALU.not_equal, fill=1.0,
                               base=0, pattern=[[-1, P]], channel_multiplier=1).then_inc(s_const, 1)
            pool.memset(ones2[:, :].bitcast(F32), 1.0).then_inc(s_const, 1)
            pool.memset(zero_idx[:, :], 0).then_inc(s_const, 1)
            pool.memset(h2_hi[:, :, :, H:HC].bitcast(F32), 1.0).then_inc(s_const, 1)
            pool.iota(node_id[:, :], pattern=[[P, NW]], base=0, channel_multiplier=1,
                      allow_small_or_imprecise_dtypes=True).then_inc(s_const, 1)
            pool.iota(first_node[:, :], pattern=[[P, NW]], base=0, channel_multiplier=0,
                      allow_small_or_imprecise_dtypes=True).then_inc(s_const, 1)
            pool.iota(iota16[:, :, :], pattern=[[0, TB], [1, P]], base=0, channel_multiplier=0,
                      allow_small_or_imprecise_dtypes=True).then_inc(s_const, 1)
            pool.memset(win_row[0:1, 0:4], 0).then_inc(s_const, 1)
            pool.memset(win_row[0:1, 4 + 2 * NB:2 * (NB + 8)], 0).then_inc(s_const, 1)

            pool.wait_ge(s_edges, 16 * len(loads))
            pool.tensor_copy(edges_f[0:BG, :], edges_in[0:BG, :]).then_inc(s_ef, 1)
            pool.tensor_copy(edges16[0:BG, :], edges_in[0:BG, 0:GR * EB]).then_inc(s_d16, 1)

            pool.wait_ge(s_xt, NG - 2)
            pool.memset(x_slot[:, (NG - 1) % 2, size(NG - 1) - 1, :], 0.0).then_inc(s_xz, 1)
            for k in range(2):
                pool.wait_ge(s_as[k], 16 * ((NG + 1 - k) // 2))
            pool.wait_ge(s_ec, GR)

            copied = pool.alloc_register("blocks_with_indices")
            pool.reg_mov(copied, 1)

            def copy_idx(i, k):
                at = k % R * TB
                v = src_idx[:, bass.ds(i * (U * TB) + k * TB, TB)]
                pool.tensor_tensor(idx_now[:, at:at + TB], v, zero_idx[:, :], ALU.add).then_inc(s_idx, 1)

            copy_idx(0, 0)

            def body(i):
                for k in range(U):
                    if there(i, k - R):
                        pool.wait_ge(s_ta, i * U + (k - R + 1))
                    if there(i, k + 1 - R):
                        for t in range(TB):
                            pool.wait_ge(s_g[(k + 1) % R * TB + t], uses(i, k + 1) * 16)
                    if there(i, k + 1):
                        pool.wait_ge(s_idx, copied)
                        copy_idx(i, k + 1)
                    else:
                        pool.wait_ge(s_idx, NB)
                    pool.reg_add(copied, copied, 1)
                    for t in range(k % R * TB, (k % R + 1) * TB):
                        pool.indirect_dma_start(a_edge[:, t, :], None, a_table,
                                                bass.IndirectOffsetOnAxis(ap=idx_now[:, t:t + 1], axis=0)
                                                ).then_inc(s_g[t], 16)
            bodies(pool, body)
            pool.wait_ge(s_h1h, NB)
            pool.memset(f_x[:, NW - 1, :], 0.0).then_inc(s_fz, 1)
            pool.wait_ge(s_fx[0], 16)

            def final(g, k, half):
                if used(g):
                    pool.wait_ge(s_fmt, g - 1)
                if isinstance(g, int) and g == 2:
                    pool.wait_ge(s_fx[1], 32)
                n = size(g)
                pool.tensor_copy(f_xs[:, k, 0:n, :], f_x[:, bass.ds(g * GW, n), :]).then_inc(s_fxs, 1)
            groups(pool, final, 0, peel=1)

        @block.scalar
        def _(act):
            act.dma_start(w_stage[:, 0:2 * H].rearrange("p (k h) -> p k h", k=2),
                          Wm1.rearrange("(k p) h -> p k h", p=P)).then_inc(s_w, 16)
            act.dma_start(rows_in[0:2, 0:H], bm1.partition_broadcast(2)).then_inc(s_w, 16)
            act.dma_start(rows_in[0:2, H:H + D], bm3.partition_broadcast(2)).then_inc(s_w, 16)
            act.dma_start(rows_in[0:2, H + D:H + 2 * D], bn2.partition_broadcast(2)).then_inc(s_w, 16)
            act.dma_start(w_stage[:, 2 * H:4 * H].rearrange("p (k h) -> p k h", k=2),
                          Wm2.rearrange("(k p) h -> p k h", p=P)).then_inc(s_w2in, 16)
            for t in range(TB):
                act.dma_start(b2_bc[:, t, :], bm2.partition_broadcast(P)).then_inc(s_b2, 16)
            act.wait_ge(s_w, 64)
            act.copy(wab[:, 0, :], w_stage[:, 0:2 * H]).then_inc(s_hi, 1)
            act.copy(rows_hi[0:2, :].bitcast(F32R), rows_in[0:2, :]).then_inc(s_hi, 1)

            def tables(g, k, half):
                if isinstance(g, int) and g == 1:
                    act.wait_ge(s_w2in, 16)
                    act.copy(w2[:, 0, :, :].rearrange("p k h -> p (k h)"), w_stage[:, 2 * H:4 * H]
                             ).then_inc(s_hi, 1)
                n = size(g)
                if n:
                    act.wait_ge(s_xt, g + 1)
                    if used(g):
                        act.wait_ge(s_ab, g * 2 - 2)
                    act.copy(xh[:, k, 0:n * P], bank[k][:, 0:n * P]).then_inc(s_xh, 1)
                n = size(g, 1)
                for q in range((n + 1) // 2):
                    m = min(n - 2 * q, 2)
                    act.wait_ge(s_ab, g * 2 - 2 + (q + 1))
                    if used(g, 1) and q == 0:
                        act.wait_ge(s_as[1 - k], ((g - 1) // 2 if isinstance(g, int) else half - 1 + k) * 16)
                    act.copy(a_out[:, 1 - k, 2 * q:2 * q + m, :],
                             bank[2 + q][:, 0:m * H].rearrange("p (w h) -> p w h", h=H)).then_inc(s_ac, 1)
                    act.copy(b_tab[:, bass.ds(g * GW - GW + 2 * q, m), 0, :].bitcast(F32R),
                             bank[4 + q][:, 0:m * H].rearrange("p (w h) -> p w h", h=H)).then_inc(s_bh, 1)
            groups(act, tables, 1)
            act.wait_ge(s_w2s, 1)
            for k in range(2):
                act.wait_ge(s_as[k], 16 * ((NG + 1 - k) // 2))
            act.copy(agg[:, zero_by_dve:], zero_idx[:, 0:1].bitcast(F32).to_broadcast([P, NW * HC - zero_by_dve])
                     ).then_inc(s_zero, 1)
            act.wait_ge(s_b2, 32)
            act.wait_ge(s_bits, 2)
            act.wait_ge(s_bl, NPAIR)
            act.wait_ge(s_row, 16)
            more = act.alloc_register("further_windows_act")
            act.reg_mov(more, 1)

            def copy_b(slot, w):
                act.copy(b_win[:, slot, :, :].rearrange("p a h -> p (a h)"),
                         b_tab[:, bass.ds(w, 1), :, :].rearrange("p o a h -> p (o a h)")
                         ).then_inc(s_bw[slot // MORE], 1)

            def copy_further_b(w):
                act.wait_ge(s_ex[1], more)
                act.reg_add(more, more, 1)
                copy_b(MORE, w)

            def copy_second_b(lo, hi):
                with act.If(lo < hi):
                    copy_further_b(after(lo))

            def copy_other_b(lo, hi):
                with act.If(lo + 1 < hi):
                    with act.Fori(lo + 2, hi + 1) as w:
                        copy_further_b(w)

            def body(i):
                win = load_windows(act, i)
                if isinstance(i, int) and i == 0:
                    copy_b(0, win[0][0])
                    copy_second_b(*win[0])
                    copy_other_b(*win[0])
                for k in steps(i):
                    if there(i, k):
                        if there(i, k + 1):
                            if there(i, k - 1):
                                act.wait_ge(s_ex[0], i * U + k)
                            copy_b((k + 1) % 2, win[k + 1][0])
                        act.wait_ge(s_ex[0], i * U + (k + 1))
                        act.wait_ge(s_ex[1], more)
                        act.activation(h1[:, k % 2, 0, :], bank[k % 2][:, :], ACT.Relu).then_inc(s_h1h, 1)
                        if there(i, k + 1):
                            copy_second_b(*win[k + 1])
                        if there(i, k - 2):
                            act.wait_ge(s_h2l, i * U + (k - 1))
                        act.copy(bank[2 + k % 2][:, :], b2_bc[:, :, :].rearrange("p t h -> p (t h)")
                                 ).then_inc(s_seed, 1)
                    if there(i, k - 1):
                        act.wait_ge(s_w2, i * U + k)
                        act.activation(h2_hi[:, (k - 1) % 2, :, 0:H],
                                       bank[2 + (k - 1) % 2][:, :].rearrange("p (t h) -> p t h", t=TB),
                                       ACT.Relu).then_inc(s_h2h, 1)
                    if there(i, k) and there(i, k + 1):
                        copy_other_b(*win[k + 1])
            bodies(act, body)

            def final(g, k, half):
                n = size(g, 1)
                if n:
                    act.wait_ge(s_fg, g)
                    if used(g, 1):
                        act.wait_ge(s_fh, g - 2)
                    act.copy(f_msg[:, 1 - k, 0:n * P], bank[4][:, 0:n * P]).then_inc(s_fa, 1)
                n = size(g)
                if n:
                    act.wait_ge(s_fmt, g + 1)
                    if used(g):
                        act.wait_ge(s_fg, g - 1)
                    act.copy(f_feat[:, k, 0, 0:n * P], bank[0][:, 0:n * P]).then_inc(s_fc, 1)
                n = size(g, 2)
                if n:
                    act.wait_ge(s_fh, g - 1)
                    if used(g, 2):
                        act.wait_ge(s_fu, g - 3)
                    for h in range(KH):
                        act.activation(f_hid[:, k, h, 0:n * P], bank[5 + h][:, 0:n * P],
                                       ACT.Relu, bias=bn1_col[:, h:h + 1]).then_inc(s_fhr, 1)
                n = size(g)
                if n:
                    act.copy(f_feat[:, k, 2, 0:n * P], bank[2][:, 0:n * P]).then_inc(s_fcx, 1)
                n = size(g, 4)
                if n:
                    act.wait_ge(s_fe, g - 3)
                    act.activation(f_sd[:, k, 0:n], f_ve[:, k, 0:n], ACT.Sqrt).then_inc(s_fs, 1)
            groups(act, final, 4)

        @block.vector
        def _(dve):
            dve.wait_ge(s_const, 9)
            dve.wait_ge(s_hi, 2)
            dve.tensor_tensor(wab[:, 1, :], w_stage[:, 0:2 * H], wab[:, 0, :].bitcast(F32), ALU.subtract
                              ).then_inc(s_split, 1)
            dve.tensor_tensor(rows_lo[0:2, :], rows_in[0:2, :], rows_hi[0:2, :], ALU.subtract
                              ).then_inc(s_lo, 1)
            dve.wait_ge(s_lo, 1)
            dve.tensor_scalar(rows_hi[0:2, :], rows_hi[0:2, :], ident[0:2, 0:1], None, ALU.mult
                              ).then_inc(s_lo, 1)
            dve.wait_ge(s_lo, 2)
            for to, a in ([(b1_rows[:, j * H:(j + 1) * H], slice(0, H)) for j in range(2)]
                          + [(b3_rows[:, :], slice(H, H + D))]
                          + [(bn2_rows[:, :], slice(H + D, H + 2 * D))]):
                dve.scalar_tensor_tensor(to, rows_lo[0:2, a], ident[0:2, 1:2], rows_hi[0:2, a],
                                         ALU.mult, ALU.add).then_inc(s_split, 1)
            def split_w2():
                dve.wait_ge(s_hi, 3)
                dve.tensor_tensor(w2[:, 1, :, :].rearrange("p k h -> p (k h)"), w_stage[:, 2 * H:4 * H],
                                  w2[:, 0, :, :].rearrange("p k h -> p (k h)").bitcast(F32), ALU.subtract
                                  ).then_inc(s_w2s, 1)

            def find_windows():
                dve.wait_ge(s_ef, 1)
                dst_f = edges_f[0:BG, 0:GR * EB].rearrange("b (g e) -> b g e", g=GR)
                for n, op in enumerate((ALU.min, ALU.max)):
                    dve.tensor_reduce(minmax[0:BG, n:2 * GR:2], dst_f, AX.X, op).then_inc(s_mm, 1)
                dve.wait_ge(s_mm, 2)
                dve.tensor_copy(minmax_i[0:BG, :], minmax[0:BG, :]).then_inc(s_wi, 1)
                dve.wait_ge(s_wi, 1)
                dve.tensor_single_scalar(win_i[0:BG, :], minmax_i[0:BG, :], 7, ALU.arith_shift_right
                                         ).then_inc(s_win, 1)

            def tables(g, k, half):
                if isinstance(g, int) and g == 1:
                    split_w2()
                if isinstance(g, int) and g == 2:
                    find_windows()
                n = size(g)
                if n:
                    dve.wait_ge(s_xh, g + 1)
                    dve.tensor_tensor(xl[:, k, 0:n * P], bank[k][:, 0:n * P], xh[:, k, 0:n * P].bitcast(F32),
                                      ALU.subtract).then_inc(s_xl, 1)
                n = size(g, 1)
                for q in range((n + 1) // 2):
                    m = min(n - 2 * q, 2)
                    dve.wait_ge(s_bh, g * 2 - 2 + (q + 1))
                    both = b_tab[:, bass.ds(g * GW - GW + 2 * q, m), :, :]
                    dve.tensor_tensor(both[:, :, 1, :], bank[4 + q][:, 0:m * H].rearrange("p (w h) -> p w h", h=H),
                                      both[:, :, 0, :], ALU.subtract).then_inc(s_bl, 1)
            groups(dve, tables, 1)
            for n, col in enumerate((src_idx, dst_col)):
                for g in range(GR):
                    dve.wait_ge(s_et, n * GR + g + 1)
                    dve.tensor_copy(col[:, g * BG * TB:(g + 1) * BG * TB].rearrange("p (b t) -> p t b", t=TB),
                                    bank[n * GR + g][:, 0:TB * BG].rearrange("p (t b) -> p t b", t=TB)
                                    ).then_inc(s_ec, 1)
            dve.wait_ge(s_ec, 2 * GR)
            dve.wait_ge(s_bl, NPAIR)
            dve.wait_ge(s_scr, 32 * GR)
            dve.wait_ge(s_row, 16)
            more_t = dve.alloc_register("further_windows_expand")
            more = dve.alloc_register("further_windows_sum")
            dve.reg_mov(more_t, 1)
            dve.reg_mov(more, 0)

            def make_onehot_t(slot, k, w):
                at = k % 2 * EB
                dve.tensor_scalar(onehot_t[:, slot, :], dst_all[:, k // 2 % 2, at:at + EB],
                                  node_id[:, bass.ds(w, 1)], None, ALU.is_equal).then_inc(s_ot[slot // MORE], 1)

            def make_further_onehot_t(k, w):
                dve.wait_ge(s_ex[1], more_t)
                dve.reg_add(more_t, more_t, 1)
                make_onehot_t(MORE, k, w)

            def make_second_onehot_t(k, lo, hi):
                with dve.If(lo < hi):
                    make_further_onehot_t(k, after(lo))

            def make_other_onehot_t(k, lo, hi):
                with dve.If(lo + 1 < hi):
                    with dve.Fori(lo + 2, hi + 1) as w:
                        make_further_onehot_t(k, w)

            def make_onehot(slot, i, k, w):
                dve.scalar_tensor_tensor(
                    onehot[:, slot, :, :], iota16[:, :, :], first_node[:, bass.ds(w, 1)],
                    dst_col[:, bass.ds(i * (U * TB) + k * TB, TB)].unsqueeze(2).to_broadcast([P, TB, P]),
                    ALU.add, ALU.is_equal).then_inc(s_oh[slot // MORE], 1)

            def make_further_onehot(i, k, w):
                dve.reg_add(more, more, 1)
                make_onehot(MORE, i, k, w)

            def add_sums(slot, w):
                sums = agg[:, bass.ds(w * HC, HC)]
                return dve.tensor_tensor(sums, bank[4 + slot][:, 0:HC], sums, ALU.add)

            def body(i):
                win = load_windows(dve, i)
                if isinstance(i, int) and i == 0:
                    dve.wait_ge(s_da[0], 16)
                    make_onehot_t(0, 0, win[0][0])
                    make_second_onehot_t(0, *win[0])
                    make_other_onehot_t(0, *win[0])
                    dve.memset(agg[:, 0:zero_by_dve], 0.0).then_inc(s_zero, 1)
                    dve.wait_ge(s_zero, 2)
                for k in steps(i):
                    if there(i, k):
                        if there(i, k + 1):
                            if (k + 1) % 2 == 0:
                                dve.wait_ge(s_da[(k + 1) // 2 % 2], uses(i, k + 1) * 16 + 16)
                            if there(i, k - 1):
                                dve.wait_ge(s_ex[0], i * U + k)
                            make_onehot_t((k + 1) % 2, k + 1, win[k + 1][0])
                        dve.wait_ge(s_h1h, i * U + (k + 1))
                        dve.scalar_tensor_tensor(h1[:, k % 2, 1, :], bank[k % 2][:, :], 0.0,
                                                 h1[:, k % 2, 0, :].bitcast(F32), ALU.max, ALU.subtract
                                                 ).then_inc(s_h1l, 1)
                        if there(i, k + 1):
                            make_second_onehot_t(k + 1, *win[k + 1])
                    if there(i, k - 1):
                        make_onehot((k - 1) % 2, i, k - 1, win[k - 1][0])
                        dve.wait_ge(s_h2h, i * U + k)
                        dve.scalar_tensor_tensor(h2_lo[:, (k - 1) % 2, :, :],
                                                 bank[2 + (k - 1) % 2][:, :].rearrange("p (t h) -> p t h", t=TB),
                                                 0.0, h2_hi[:, (k - 1) % 2, :, 0:H].bitcast(F32),
                                                 ALU.max, ALU.subtract).then_inc(s_h2l, 1)
                    if there(i, k - 2):
                        lo, hi = win[k - 2]
                        with dve.If(lo < hi):
                            if there(i, k - 3):
                                dve.wait_ge(s_add, i * U + (k - 2))
                            dve.wait_ge(s_sg[1], more)
                            add_sums(MORE, after(lo))
                            with dve.If(lo + 1 < hi):
                                with dve.Fori(lo + 2, hi + 1) as w:
                                    make_further_onehot(i, k - 2, w)
                                    dve.wait_ge(s_sg[1], more)
                                    add_sums(MORE, w)
                        if there(i, k - 3):
                            dve.wait_ge(s_add, i * U + (k - 2))
                        dve.wait_ge(s_sg[0], i * U + (k - 1))
                        add_sums(k % 2, lo).then_inc(s_add, 1)
                    if there(i, k - 1):
                        lo, hi = win[k - 1]
                        with dve.If(lo < hi):
                            make_further_onehot(i, k - 1, after(lo))
                    if there(i, k) and there(i, k + 1):
                        make_other_onehot_t(k + 1, *win[k + 1])
            bodies(dve, body)
            dve.wait_ge(s_add, NB)

            agg3 = agg[:, :].rearrange("p (w c) -> p w c", c=HC)

            def reciprocal_counts(g, k, n):
                dve.tensor_scalar(f_cnt[:, k, 0:n], agg3[:, bass.ds(g * GW, n), H:H + 1]
                                  .rearrange("p w o -> p (w o)"), 1.0, None, ALU.max).then_inc(s_f1, 1)
                dve.wait_ge(s_f1, g + 1)
                dve.reciprocal(f_rec[:, k, 0:n], f_cnt[:, k, 0:n]).then_inc(s_f2, 1)

            def means(g, k, n):
                for j in range(n):
                    ins = dve.tensor_scalar(f_mean[:, k, j, :], agg[:, bass.ds((g * GW + j) * HC, HC)],
                                            f_rec[:, k, j:j + 1], None, ALU.mult)
                ins.then_inc(s_fm, 1)

            reciprocal_counts(0, 0, size(0))
            dve.wait_ge(s_f2, 1)
            means(0, 0, size(0))
            def final(g, k, half):
                ahead = size(g, -1)
                if ahead:
                    reciprocal_counts(g + 1, 1 - k, ahead)
                n = size(g, 4)
                if n:
                    dve.wait_ge(s_fu, g - 3)
                    if used(g, 4):
                        dve.wait_ge(s_fo, g - 5)
                    if isinstance(g, int) and g == 4:
                        for q in range(2):
                            dve.wait_ge(s_fx[q], 16 * (q + 1))
                    y = f_y[:, k, 0:n * D]
                    dve.scalar_tensor_tensor(y.rearrange("p (w d) -> p w d", d=D),
                                             f_x[:, bass.ds(g * GW - 4 * GW, n), :], 2.0,
                                             bank[7][:, 0:n * D].rearrange("p (w d) -> p w d", d=D),
                                             ALU.mult, ALU.add).then_inc(s_fy, 1)
                    dve.wait_ge(s_fy, g - 3)
                    for j in range(n):
                        dve.bn_stats(f_bn[:, k, j, :], y[:, j * D:(j + 1) * D]).then_inc(s_fn, 1)
                    if n < GW or isinstance(g, int):
                        dve.wait_ge(s_fn, GW * (g - 4) + n)
                    else:
                        dve.wait_ge(s_fn, g * GW - 3 * GW)
                if ahead:
                    dve.wait_ge(s_f2, g + 2)
                    if used(g, -1):
                        dve.wait_ge(s_fmt, g)
                    means(g + 1, 1 - k, ahead)
                if n:
                    for j in range(n):
                        dve.bn_aggr(f_mv[:, k, j, :], f_bn[:, k, j, :]).then_inc(s_fv, 1)
                    if n < GW or isinstance(g, int):
                        dve.wait_ge(s_fv, GW * (g - 4) + n)
                    else:
                        dve.wait_ge(s_fv, g * GW - 3 * GW)
                    dve.tensor_scalar(f_ve[:, k, 0:n], f_mv[:, k, 0:n, 1:2].rearrange("p w o -> p (w o)"),
                                      EPS, None, ALU.add).then_inc(s_fe, 1)
                n = size(g)
                if n:
                    dve.wait_ge(s_fmt, g + 1)
                    if used(g):
                        dve.wait_ge(s_fg, g - 1)
                    dve.tensor_copy(f_feat[:, k, 1, 0:n * P], bank[1][:, 0:n * P])
                    dve.tensor_copy(f_row[k][:, 0:n * P], bank[3][0:2, 0:n * P]).then_inc(s_fr, 1)
                n = size(g, 5)
                if n:
                    j = 1 - k
                    dve.wait_ge(s_fs, g - 4)
                    dve.reciprocal(f_rs[:, j, 0:n], f_sd[:, j, 0:n]).then_inc(s_fq, 1)
                    dve.wait_ge(s_fq, g - 4)
                    if used(g, 5):
                        dve.wait_ge(s_fst[j], ((g - 5) // 2 if isinstance(g, int) else half - 3 + k) * 16)
                    for w in range(n):
                        ins = dve.tensor_scalar(f_out[:, j, w, :], f_y[:, j, w * D:(w + 1) * D],
                                                f_mv[:, j, w, 0:1], f_rs[:, j, w:w + 1], ALU.subtract, ALU.mult)
                    ins.then_inc(s_fo, 1)
            groups(dve, final, 5, 1)

        @block.tensor
        def _(pe):
            pe.wait_ge(s_const, 9)

            def tables(g, k, half):
                n = size(g)
                if n:
                    extra = 1 if n < GW and n > 1 else 0
                    pe.wait_ge(s_xs[k], 16 * (half + 1 + extra))
                    if used(g):
                        pe.wait_ge(s_xl, g - 1)
                    for j in range(n):
                        ins = pe.transpose(bank[k][:, j * P:(j + 1) * P], x_slot[:, k, j, :], ident[:, :])
                    ins.then_inc(s_xt, 1)
                if isinstance(g, int) and g == 1:
                    pe.wait_ge(s_split, 5)
                n = size(g, 1)
                if n:
                    pe.wait_ge(s_xl, g)
                for q in range((n + 1) // 2):
                    m = min(n - 2 * q, 2)
                    if used(g, 0):
                        pe.wait_ge(s_ac, g * 2 - 4 + (q + 1))
                        pe.wait_ge(s_bl, g * 2 - 4 + (q + 1))
                    pe.matmul(bank[4 + q][:, 0:m * H], ones2[:, :], b1_rows[:, 0:m * H], start=True, stop=False,
                              skip_group_check=True)
                    for w in range(m):
                        v = slice((2 * q + w) * P, (2 * q + w + 1) * P)
                        for c in range(2):
                            for n_, (xp, a) in enumerate(((xh, 0), (xh, 1), (xl, 0))):
                                ins = pe.matmul(bank[2 + 2 * c + q][:, w * H:(w + 1) * H], xp[:, 1 - k, v],
                                                wab[:, a, c * H:(c + 1) * H],
                                                start=(c == 0 and w == 0 and n_ == 0), stop=(n_ == 2),
                                                skip_group_check=True)
                    ins.then_inc(s_ab, 1)
            groups(pe, tables, 1)
            pe.wait_ge(s_ef, 1)
            pe.wait_ge(s_ac, NPAIR)
            pe.wait_ge(s_bl, NPAIR)
            for n in range(2):
                for g in range(GR):
                    for t in range(TB):
                        at = ((1 - n) * GR + g) * EB + t * P
                        ins = pe.transpose(bank[n * GR + g][:, t * BG:(t + 1) * BG], edges_f[0:BG, at:at + P],
                                           ident[0:BG, 0:BG])
                    ins.then_inc(s_et, 1)
            pe.wait_ge(s_row, 16)
            pe.wait_ge(s_ec, 2 * GR)
            pe.wait_ge(s_w2s, 1)
            for k in range(2):
                pe.matmul(bank[2 + k][:, :], ones2[:, :], w2[0:2, 0, :, :].rearrange("p k h -> p (k h)"),
                          start=True, stop=True).then_inc(s_bits, 1)
            more_t = pe.alloc_register("further_windows_expand_pe")
            more = pe.alloc_register("further_windows_sum_pe")
            pe.reg_mov(more_t, 0)
            pe.reg_mov(more, 0)
            pe.nop().then_inc(s_ex[1], 1)

            def expand(slot, k):
                for h in range(KH):
                    for a in range(2):
                        ins = pe.matmul(bank[k % 2][:, h * EB:(h + 1) * EB], b_win[:, slot, a, h * P:(h + 1) * P],
                                        onehot_t[:, slot, :], start=False, stop=True, skip_group_check=True)
                ins.then_inc(s_ex[slot // MORE], 1)

            def expand_further(k):
                pe.reg_add(more_t, more_t, 1)
                pe.wait_ge(s_ot[1], more_t)
                pe.wait_ge(s_bw[1], more_t)
                expand(MORE, k)

            def sum_segments(slot, k):
                to = bank[4 + slot]
                for t in range(TB):
                    pe.matmul(to[:, 0:HC], onehot[:, slot, t, :], h2_hi[:, k % 2, t, :], start=(t == 0),
                              stop=False, skip_group_check=True)
                    ins = pe.matmul(to[:, 0:H], onehot[:, slot, t, :], h2_lo[:, k % 2, t, :], start=False,
                                    stop=(t == TB - 1), skip_group_check=True)
                ins.then_inc(s_sg[slot // MORE], 1)

            def sum_further(k):
                pe.reg_add(more, more, 1)
                pe.wait_ge(s_oh[1], more)
                sum_segments(MORE, k)

            def body(i):
                win = load_windows(pe, i)
                for k in steps(i):
                    if there(i, k):
                        for t in range(TB):
                            pe.wait_ge(s_g[k % R * TB + t], uses(i, k) * 16 + 16)
                            for h in range(KH):
                                ins = pe.matmul(bank[k % 2][:, h * EB + t * P:h * EB + (t + 1) * P],
                                                a_edge[:, k % R * TB + t, h * P:(h + 1) * P], ident[:, :],
                                                start=(t == 0 and h == 0), stop=False, is_transpose=True,
                                                skip_group_check=True)
                        ins.then_inc(s_ta, 1)
                        pe.wait_ge(s_ot[0], i * U + (k + 1))
                        pe.wait_ge(s_bw[0], i * U + (k + 1))
                        expand(k % 2, k)
                        further(pe, *win[k], lambda w: expand_further(k))
                    if there(i, k - 1):
                        j = (k - 1) % 2
                        pe.wait_ge(s_seed, i * U + k)
                        pe.wait_ge(s_h1l, i * U + k)
                        for t in range(TB):
                            to = bank[2 + j][:, t * H:(t + 1) * H]
                            for a, b in ((0, 0), (0, 1), (1, 0)):
                                for h in range(KH):
                                    ins = pe.matmul(to, h1[:, j, a, h * EB + t * P:h * EB + (t + 1) * P],
                                                    w2[:, b, h, :], start=False, stop=(a == 1 and h == KH - 1),
                                                    skip_group_check=True)
                        ins.then_inc(s_w2, 1)
                    if there(i, k - 2):
                        pe.wait_ge(s_h2l, i * U + (k - 1))
                        pe.wait_ge(s_oh[0], i * U + (k - 1))
                        sum_segments(k % 2, k - 2)
                        further(pe, *win[k - 2], lambda w: sum_further(k - 2))
            bodies(pe, body)
            pe.wait_ge(s_fw, 16 * (3 + KH))

            def final(g, k, half):
                n = size(g)
                if n:
                    pe.wait_ge(s_fm, g + 1)
                    pe.wait_ge(s_fxs, g + 1)
                    if not isinstance(g, int) or g >= 1:
                        pe.wait_ge(s_fcx, g)
                        pe.wait_ge(s_fr, g)
                    for w in range(n):
                        v = slice(w * P, (w + 1) * P)
                        for h in range(KH):
                            pe.transpose(bank[h][:, v], f_mean[:, k, w, h * P:(h + 1) * P], ident[:, :])
                        pe.transpose(bank[2][:, v], f_xs[:, k, w, :], ident[:, :])
                        ins = pe.transpose(bank[3][0:2, v], f_mean[:, k, w, H:HC], ident[:, :])
                    ins.then_inc(s_fmt, 1)
                j = 1 - k
                n = size(g, 1) * P
                if n:
                    pe.wait_ge(s_fc, g)
                    pe.wait_ge(s_fr, g)
                    if used(g):
                        pe.wait_ge(s_fa, g - 1)
                    for h in range(KH):
                        pe.matmul(bank[4][:, 0:n], w3[:, h, :], f_feat[:, j, h, 0:n], start=(h == 0), stop=False)
                    pe.matmul(bank[4][:, 0:n], b3_rows[:, :], f_row[j][:, 0:n], start=False, stop=True
                              ).then_inc(s_fg, 1)
                n = size(g, 2) * P
                if n:
                    pe.wait_ge(s_fa, g - 1)
                    pe.wait_ge(s_fcx, g - 1)
                    if used(g, 1):
                        pe.wait_ge(s_fhr, g * 2 - 4)
                    for h in range(KH):
                        to = bank[5 + h][:, 0:n]
                        pe.matmul(to, wn1[:, 0, h * P:(h + 1) * P], f_feat[:, k, 2, 0:n], start=True, stop=False)
                        ins = pe.matmul(to, wn1[:, 1, h * P:(h + 1) * P], f_msg[:, k, 0:n], start=False, stop=True)
                    ins.then_inc(s_fh, 1)
                n = size(g, 3)
                if n:
                    pe.wait_ge(s_fhr, g * 2 - 4)
                    if used(g, 2):
                        pe.wait_ge(s_fy, g - 3)
                    pe.matmul(bank[7][:, 0:n * D].rearrange("p (w d) -> p w d", d=D), ones2[:, :],
                              bn2_rows[:, :].unsqueeze(1).to_broadcast([2, n, D]), start=True, stop=False,
                              skip_group_check=True)
                    for w in range(n):
                        for h in range(KH):
                            ins = pe.matmul(bank[7][:, w * D:(w + 1) * D], f_hid[:, j, h, w * P:(w + 1) * P],
                                            wn2[:, h, :], start=False, stop=(h == KH - 1), skip_group_check=True)
                    ins.then_inc(s_fu, 1)
            groups(pe, final, 3)


_INS = ["x", "src", "dst"] + ["L0_gnn_" + n for n in
                              ("Wm1", "bm1", "Wm2", "bm2", "Wm3", "bm3", "Wn1", "bn1", "Wn2", "bn2")]


def kernel(**inputs):
    import numpy as np
    import concourse.bacc as bacc
    from concourse.bass_utils import run_bass_kernel_spmd

    nc = bacc.Bacc("TRN2", target_bir_lowering=False, num_devices=1)
    arrays, args = {}, []
    for name in _INS:
        a = np.ascontiguousarray(inputs[name])
        arrays[f"in_{name}"] = a
        args.append(nc.dram_tensor(f"in_{name}", a.shape, mybir.dt.from_np(a.dtype), kind="ExternalInput").ap())
    shape = inputs["x"].shape
    args.append(nc.dram_tensor("out_0", shape, F32, kind="ExternalOutput").ap())
    gnn_layer(nc, *args)
    r = run_bass_kernel_spmd(nc, [arrays], core_ids=[0])
    return r.results[0]["out_0"]
```
